# Optimizing a Trainium2 kernel written in Bass

```python
import numpy as np
import jax
import jax.numpy as jnp

def _softmax(x, axis=-1):
    return jax.nn.softmax(x, axis=axis)

def _gelu(x):
    return jax.nn.gelu(x, approximate=True)

def _silu(x):
    return jax.nn.silu(x)

def _sigmoid(x):
    return jax.nn.sigmoid(x)

def _layernorm(x, axis=-1, eps=1e-05):
    m = jnp.mean(x, axis=axis, keepdims=True)
    v = jnp.var(x, axis=axis, keepdims=True)
    return (x - m) / jnp.sqrt(v + eps)

def _scatter_add(tgt, idx, src, axis=0):
    return tgt.at[idx].add(src)

def _segment_sum(src, seg, n):
    return jax.ops.segment_sum(src, seg, n)
kernel_name = 'mk_hybrid_d1_jaxref_r8_28cec6'

def setup_inputs(seed: int=0):
    np.random.seed(seed)
    _w = jnp.asarray

    def _L0_attn_a_setup():
        import jax, jax.numpy as jnp
        import numpy as np
        B, T, D, L, K = (4, 256, 256, 256, 4)

        def _reference_tuple_inner(x, w_y, b_y, w_x, b_x, conv_w, conv_b, a_param, w_ig, b_ig, w_ag, b_ag, w_out, b_out):
            Tn = x.shape[1]
            y = jax.nn.gelu(jnp.einsum('btd,dl->btl', x, w_y) + b_y, approximate=False)
            xb = jnp.einsum('btd,dl->btl', x, w_x) + b_x
            xp = jnp.pad(xb, ((0, 0), (K - 1, 0), (0, 0)))
            conv = conv_b
            for k in range(K):
                conv = conv + conv_w[k] * xp[:, k:k + Tn]
            gate_x = jax.nn.sigmoid(jnp.einsum('btl,lm->btm', conv, w_ig) + b_ig)
            gate_a = jax.nn.sigmoid(jnp.einsum('btl,lm->btm', conv, w_ag) + b_ag)
            log_a = -8.0 * gate_a * jax.nn.softplus(a_param)
            a = jnp.exp(log_a)
            mult = jnp.sqrt(1.0 - jnp.exp(2.0 * log_a))
            reset = (jnp.arange(Tn) == 0)[None, :, None]
            a = jnp.where(reset, 0.0, a)
            mult = jnp.where(reset, 1.0, mult)
            nx = gate_x * conv * mult

            def step(h, inp):
                a_t, x_t = inp
                h = a_t * h + x_t
                return (h, h)
            h0 = jnp.zeros((x.shape[0], a.shape[-1]), x.dtype)
            hn, hs = jax.lax.scan(step, h0, (a.transpose(1, 0, 2), nx.transpose(1, 0, 2)))
            h_seq = hs.transpose(1, 0, 2)
            out = jnp.einsum('btl,ld->btd', h_seq * y, w_out) + b_out
            return (out, hn)
        key = jax.random.key(seed)
        ks = jax.random.split(key, 12)
        s = 0.02
        f32 = jnp.float32
        return {'x': jax.random.normal(ks[0], (B, T, D), f32), 'w_y': jax.random.normal(ks[1], (D, L), f32) * s, 'b_y': jnp.zeros((L,), f32), 'w_x': jax.random.normal(ks[2], (D, L), f32) * s, 'b_x': jnp.zeros((L,), f32), 'conv_w': jax.random.normal(ks[3], (K, L), f32) * s, 'conv_b': jnp.zeros((L,), f32), 'a_param': jax.random.uniform(ks[4], (L,), f32, 0.5, 4.0), 'w_ig': jax.random.normal(ks[5], (L, L), f32) * s, 'b_ig': jnp.zeros((L,), f32), 'w_ag': jax.random.normal(ks[6], (L, L), f32) * s, 'b_ag': jnp.zeros((L,), f32), 'w_out': jax.random.normal(ks[7], (L, D), f32) * s, 'b_out': jnp.zeros((D,), f32)}
    _L0_attn_a_in = _L0_attn_a_setup()

    def _L0_attn_b_setup():
        import jax, jax.numpy as jnp
        import numpy as np
        EPS = 1e-08

        def _l2norm(v):
            return v / (jnp.linalg.norm(v, axis=-1, keepdims=True) + EPS)
        key = jax.random.key(seed)
        k1, k2, k3, k4 = jax.random.split(key, 4)
        B, T, C = (2, 256, 256)
        scale = 1.0 / np.sqrt(C)
        return {'x': jax.random.normal(k1, (B, T, C), dtype=jnp.float32), 'wq': jax.random.normal(k2, (C, C), dtype=jnp.float32) * scale, 'wk': jax.random.normal(k3, (C, C), dtype=jnp.float32) * scale, 'wv': jax.random.normal(k4, (C, C), dtype=jnp.float32) * scale, 'tau': jnp.ones((1,), dtype=jnp.float32), 'nu': jnp.ones((1,), dtype=jnp.float32)}
    _L0_attn_b_in = _L0_attn_b_setup()

    def _L0_ffn_setup():
        import jax, jax.numpy as jnp
        import numpy as np
        B, T, D, H = (4, 256, 256, 176)
        E, K = (16, 2)
        G, TKG, S = (4, 2, 1)
        SCALE = 1.0

        def _moe(x, gate_w, w1, w2, sw1, sw2):
            Bx, Tx, Dx = x.shape
            xf = x.reshape(-1, Dx)
            N = xf.shape[0]
            shared = jnp.zeros_like(xf)
            for s in range(S):
                shared = shared + jax.nn.silu(xf @ sw1[s]) @ sw2[s]
            scores = jax.nn.sigmoid(xf @ gate_w.T)
            gs = E // G
            sg = scores.reshape(N, G, gs)
            group_scores = jax.lax.top_k(sg, min(2, gs))[0].sum(axis=-1)
            _, gidx = jax.lax.top_k(group_scores, TKG)
            gmask = jax.nn.one_hot(gidx, G, dtype=scores.dtype).max(axis=1)
            masked = (sg * gmask[:, :, None]).reshape(N, E)
            tw, ti = jax.lax.top_k(masked, K)
            tw = tw / (tw.sum(axis=-1, keepdims=True) + 1e-20) * SCALE
            combine = jnp.zeros((N, E), scores.dtype).at[jnp.arange(N)[:, None], ti].add(tw)
            out = shared
            for e in range(E):
                out = out + combine[:, e:e + 1] * (jax.nn.silu(xf @ w1[e]) @ w2[e])
            return out.reshape(Bx, Tx, Dx)
        key = jax.random.key(seed)
        ks = jax.random.split(key, 6)
        x = jax.random.normal(ks[0], (B, T, D), jnp.float32)
        gate_w = jax.random.normal(ks[1], (E, D), jnp.float32) * 0.02
        w1 = jax.random.normal(ks[2], (E, D, H), jnp.float32) * 0.02
        w2 = jax.random.normal(ks[3], (E, H, D), jnp.float32) * 0.02
        sw1 = jax.random.normal(ks[4], (S, D, H), jnp.float32) * 0.02
        sw2 = jax.random.normal(ks[5], (S, H, D), jnp.float32) * 0.02
        return {'x': x, 'gate_w': gate_w, 'w1': w1, 'w2': w2, 'sw1': sw1, 'sw2': sw2}
    _L0_ffn_in = _L0_ffn_setup()
    _d = {'L0_attn_a_x': _L0_attn_a_in['x'], 'L0_attn_a_w_y': _L0_attn_a_in['w_y'], 'L0_attn_a_b_y': _L0_attn_a_in['b_y'], 'L0_attn_a_w_x': _L0_attn_a_in['w_x'], 'L0_attn_a_b_x': _L0_attn_a_in['b_x'], 'L0_attn_a_conv_w': _L0_attn_a_in['conv_w'], 'L0_attn_a_conv_b': _L0_attn_a_in['conv_b'], 'L0_attn_a_a_param': _L0_attn_a_in['a_param'], 'L0_attn_a_w_ig': _L0_attn_a_in['w_ig'], 'L0_attn_a_b_ig': _L0_attn_a_in['b_ig'], 'L0_attn_a_w_ag': _L0_attn_a_in['w_ag'], 'L0_attn_a_b_ag': _L0_attn_a_in['b_ag'], 'L0_attn_a_w_out': _L0_attn_a_in['w_out'], 'L0_attn_a_b_out': _L0_attn_a_in['b_out'], 'L0_attn_b_wq': _L0_attn_b_in['wq'], 'L0_attn_b_wk': _L0_attn_b_in['wk'], 'L0_attn_b_wv': _L0_attn_b_in['wv'], 'L0_attn_b_tau': _L0_attn_b_in['tau'], 'L0_attn_b_nu': _L0_attn_b_in['nu'], 'L0_ffn_gate_w': _L0_ffn_in['gate_w'], 'L0_ffn_w1': _L0_ffn_in['w1'], 'L0_ffn_w2': _L0_ffn_in['w2'], 'L0_ffn_sw1': _L0_ffn_in['sw1'], 'L0_ffn_sw2': _L0_ffn_in['sw2']}
    _x0 = _d['L0_attn_a_x']
    _d['L0_attn_a_x'] = jax.random.normal(jax.random.fold_in(jax.random.key(seed), 1), (4, 512, 256), dtype=_x0.dtype)
    del _x0
    return _d

def reference(L0_attn_a_x, L0_attn_a_w_y, L0_attn_a_b_y, L0_attn_a_w_x, L0_attn_a_b_x, L0_attn_a_conv_w, L0_attn_a_conv_b, L0_attn_a_a_param, L0_attn_a_w_ig, L0_attn_a_b_ig, L0_attn_a_w_ag, L0_attn_a_b_ag, L0_attn_a_w_out, L0_attn_a_b_out, L0_attn_b_wq, L0_attn_b_wk, L0_attn_b_wv, L0_attn_b_tau, L0_attn_b_nu, L0_ffn_gate_w, L0_ffn_w1, L0_ffn_w2, L0_ffn_sw1, L0_ffn_sw2):

    def _L0_attn_a_ref(x, w_y, b_y, w_x, b_x, conv_w, conv_b, a_param, w_ig, b_ig, w_ag, b_ag, w_out, b_out):
        import jax, jax.numpy as jnp
        import numpy as np
        B, T, D, L, K = (4, 256, 256, 256, 4)

        def _reference_tuple_inner(x, w_y, b_y, w_x, b_x, conv_w, conv_b, a_param, w_ig, b_ig, w_ag, b_ag, w_out, b_out):
            Tn = x.shape[1]
            y = jax.nn.gelu(jnp.einsum('btd,dl->btl', x, w_y) + b_y, approximate=False)
            xb = jnp.einsum('btd,dl->btl', x, w_x) + b_x
            xp = jnp.pad(xb, ((0, 0), (K - 1, 0), (0, 0)))
            conv = conv_b
            for k in range(K):
                conv = conv + conv_w[k] * xp[:, k:k + Tn]
            gate_x = jax.nn.sigmoid(jnp.einsum('btl,lm->btm', conv, w_ig) + b_ig)
            gate_a = jax.nn.sigmoid(jnp.einsum('btl,lm->btm', conv, w_ag) + b_ag)
            log_a = -8.0 * gate_a * jax.nn.softplus(a_param)
            a = jnp.exp(log_a)
            mult = jnp.sqrt(1.0 - jnp.exp(2.0 * log_a))
            reset = (jnp.arange(Tn) == 0)[None, :, None]
            a = jnp.where(reset, 0.0, a)
            mult = jnp.where(reset, 1.0, mult)
            nx = gate_x * conv * mult

            def step(h, inp):
                a_t, x_t = inp
                h = a_t * h + x_t
                return (h, h)
            h0 = jnp.zeros((x.shape[0], a.shape[-1]), x.dtype)
            hn, hs = jax.lax.scan(step, h0, (a.transpose(1, 0, 2), nx.transpose(1, 0, 2)))
            h_seq = hs.transpose(1, 0, 2)
            out = jnp.einsum('btl,ld->btd', h_seq * y, w_out) + b_out
            return (out, hn)
        return _reference_tuple_inner(x, w_y, b_y, w_x, b_x, conv_w, conv_b, a_param, w_ig, b_ig, w_ag, b_ag, w_out, b_out)[0]

    def _L0_attn_b_ref(x, wq, wk, wv, tau, nu):
        import jax, jax.numpy as jnp
        import numpy as np
        EPS = 1e-08

        def _l2norm(v):
            return v / (jnp.linalg.norm(v, axis=-1, keepdims=True) + EPS)
        B, T, C = x.shape
        H = 16
        D = C // H
        q = (x @ wq.T).reshape(B, T, H, D).transpose(0, 2, 1, 3)
        k = (x @ wk.T).reshape(B, T, H, D).transpose(0, 2, 1, 3)
        v = (x @ wv.T).reshape(B, T, H, D).transpose(0, 2, 1, 3)
        q, k, v = (_l2norm(q), _l2norm(k), _l2norm(v))
        scores = jnp.einsum('bhqd,bhkd->bhqk', q, k) * tau[0]
        causal = jnp.tril(jnp.ones((T, T), dtype=bool))
        scores = jnp.where(causal, scores, -jnp.inf)
        p = jax.nn.softmax(scores, axis=-1)
        out = jnp.einsum('bhqk,bhkd->bhqd', p, v)
        out = out.transpose(0, 2, 1, 3).reshape(B, T, C)
        return out * nu[0]

    def _L0_ffn_ref(x, gate_w, w1, w2, sw1, sw2):
        import jax, jax.numpy as jnp
        import numpy as np
        B, T, D, H = (4, 256, 256, 176)
        E, K = (16, 2)
        G, TKG, S = (4, 2, 1)
        SCALE = 1.0

        def _moe(x, gate_w, w1, w2, sw1, sw2):
            Bx, Tx, Dx = x.shape
            xf = x.reshape(-1, Dx)
            N = xf.shape[0]
            shared = jnp.zeros_like(xf)
            for s in range(S):
                shared = shared + jax.nn.silu(xf @ sw1[s]) @ sw2[s]
            scores = jax.nn.sigmoid(xf @ gate_w.T)
            gs = E // G
            sg = scores.reshape(N, G, gs)
            group_scores = jax.lax.top_k(sg, min(2, gs))[0].sum(axis=-1)
            _, gidx = jax.lax.top_k(group_scores, TKG)
            gmask = jax.nn.one_hot(gidx, G, dtype=scores.dtype).max(axis=1)
            masked = (sg * gmask[:, :, None]).reshape(N, E)
            tw, ti = jax.lax.top_k(masked, K)
            tw = tw / (tw.sum(axis=-1, keepdims=True) + 1e-20) * SCALE
            combine = jnp.zeros((N, E), scores.dtype).at[jnp.arange(N)[:, None], ti].add(tw)
            out = shared
            for e in range(E):
                out = out + combine[:, e:e + 1] * (jax.nn.silu(xf @ w1[e]) @ w2[e])
            return out.reshape(Bx, Tx, Dx)
        return _moe(x, gate_w, w1, w2, sw1, sw2)
    x = L0_attn_a_x
    x = x + _L0_attn_a_ref(_layernorm(x, axis=-1), L0_attn_a_w_y, L0_attn_a_b_y, L0_attn_a_w_x, L0_attn_a_b_x, L0_attn_a_conv_w, L0_attn_a_conv_b, L0_attn_a_a_param, L0_attn_a_w_ig, L0_attn_a_b_ig, L0_attn_a_w_ag, L0_attn_a_b_ag, L0_attn_a_w_out, L0_attn_a_b_out)
    x = x + _L0_ffn_ref(_layernorm(x, axis=-1), L0_ffn_gate_w, L0_ffn_w1, L0_ffn_w2, L0_ffn_sw1, L0_ffn_sw2)
    x = x + _L0_attn_b_ref(_layernorm(x, axis=-1), L0_attn_b_wq, L0_attn_b_wk, L0_attn_b_wv, L0_attn_b_tau, L0_attn_b_nu)
    x = x + _L0_ffn_ref(_layernorm(x, axis=-1), L0_ffn_gate_w, L0_ffn_w1, L0_ffn_w2, L0_ffn_sw1, L0_ffn_sw2)
    return x

_drawn_inputs = setup_inputs


def setup_inputs(seed=0):
    import zlib

    import numpy as np

    out = dict(_drawn_inputs(seed))
    spreads = {'L0_attn_a_b_y': (0.0, 0.8),
     'L0_attn_a_b_x': (0.0, 0.8),
     'L0_attn_a_conv_b': (0.0, 0.8),
     'L0_attn_a_b_ig': (0.0, 0.8),
     'L0_attn_a_b_ag': (0.0, 0.8),
     'L0_attn_a_b_out': (0.0, 0.285)}
    factors = {'L0_attn_a_w_y': 8.0,
     'L0_attn_a_w_x': 8.0,
     'L0_attn_a_conv_w': 8.0,
     'L0_attn_a_a_param': 8.0,
     'L0_attn_a_w_ig': 8.0,
     'L0_attn_a_w_ag': 8.0,
     'L0_attn_a_w_out': 8.0,
     'L0_attn_b_wq': 58.984,
     'L0_attn_b_wk': 58.64,
     'L0_ffn_gate_w': 3.513,
     'L0_ffn_w1': 3.319,
     'L0_ffn_w2': 3.308}
    for name, (base, spread) in spreads.items():
        noise = np.random.default_rng([zlib.crc32(name.encode()), seed]).standard_normal(out[name].shape)
        drawn = base * np.exp(spread * noise) if base else spread * noise
        out[name] = jnp.asarray(drawn.astype(out[name].dtype))
    for name, factor in factors.items():
        out[name] = (out[name] * factor).astype(out[name].dtype)
    return out
```

```python
from contextlib import ExitStack

import concourse.bass as bass
import numpy as np
from concourse import mybir

ALU = mybir.AluOpType
ACT = mybir.ActivationFunctionType
F32 = mybir.dt.float32
F32R = mybir.dt.float32r
BF16 = mybir.dt.bfloat16
U32 = mybir.dt.uint32
AX_X = mybir.AxisListType.X

P = 128
B, T, D = 4, 512, 256
KD = D // P
TT = T // P
L = 256
TAPS = 4
E, H, TOPK = 16, 176, 2
G = 4
GS = E // G
NCH = -(-(E + 1) * H // P)
NROUTED = E * H // P
HID = NCH * P
assert E * H == NROUTED * P
HEADS, HD = 16, 16
HH = HEADS // 2
HP = HH // 2
HW = HH * HD
PAIR = 2
LN_EPS = 1e-5
L2_EPS = 1e-8
TOP_EPS = 1e-20
NEG = -1.0e30
NVEC = 10
(V_BY, V_BX, V_CB, V_AP, V_BIG, V_BAG, V_CW) = range(7)
MATS_A = 5
M_Y, M_X, M_IG, M_AG, M_OUT = range(MATS_A)


class Count:

    def __init__(self):
        self.n = {}

    def next(self, name, by=1):
        self.n[name] = self.n.get(name, 0) + by
        return self.n[name]

    def before(self, name):
        n = self.n.get(name, 0)
        self.n[name] = n + 1
        return n


def weave(main, n_main, side, n_side):
    done = 0
    for i in range(n_main):
        next(main)
        while done * n_main < (i + 1) * n_side:
            next(side)
            done += 1
    for rest in (main, side):
        assert next(rest, "end") == "end"


def run_all(steps):
    for _ in steps:
        pass


def hybrid_kernel(nc, x, mats_a, w_qkv, gate_w, w1, w2, vecs, b_out, tau, nu, sel, out):
    ctx = ExitStack()
    with ctx:
        def sb(name, shape, dt=F32, on=ctx):
            return on.enter_context(nc.sbuf_tensor(name, shape, dt))

        sems = []

        def sem(name):
            s = ctx.enter_context(nc.semaphore(name))
            sems.append(s)
            return s

        banks = [ctx.enter_context(nc.psum_tensor(f"bank{i}", [P, 512], F32)) for i in range(8)]

        w1h = sb("w1h", [P, KD, HID], F32R)
        w1l = sb("w1l", [P, KD, HID], F32R)
        w2h = sb("w2h", [P, NCH, D], F32R)
        w2l = sb("w2l", [P, NCH, D], F32R)
        wqkv = [sb(f"wqkv{i}", [P, KD, 3 * D], F32R) for i in range(2)]
        gw = [sb(f"gw{i}", [P, KD, E], F32R) for i in range(2)]
        selr = sb("selr", [P, NROUTED * P], F32R)
        xTh = [sb(f"xTh{b}", [P, KD, T], F32R) for b in range(PAIR)]
        xTl = [sb(f"xTl{b}", [P, KD, T], F32R) for b in range(PAIR)]
        ident = sb("ident", [P, P])
        identb = sb("identb", [P, P], BF16)
        maskb = sb("maskb", [P, P], BF16)
        mv = sb("mv", [P, TT, 2])
        stats = sb("stats", [P, TT, 6])
        vare = sb("vare", [P, TT])
        rstd = sb("rstd", [P, TT])
        mhalf = sb("mhalf", [P, TT])
        phalf = sb("phalf", [P, 3 * HH])
        taub = sb("taub", [P, 1])
        nub = sb("nub", [P, 1])

        x_rows = x.rearrange("b (t p) d -> b p t d", p=P)
        out_rows = out.rearrange("b (t p) d -> b p t d", p=P)

        def clear_all():
            for s in sems:
                nc.sync.sem_clear(s)
            nc.all_engine_barrier()

        QA = B
        W1Q, W2Q = HID // QA, NCH // QA
        a_ctx = ExitStack()
        with a_ctx:
            def sba(name, shape, dt=F32):
                return sb(name, shape, dt, a_ctx)

            wa = [sba(f"wa{i}", [P, KD, MATS_A * L], F32R) for i in range(2)]
            vec = sba("vec", [P, NVEC * 2])
            nsp = sba("nsp", [P, 2])
            sp1 = sba("sp1", [P, 2])
            sp2 = sba("sp2", [P, 2])
            one = sba("one", [P, 1])
            boutb = sba("boutb", [P, D])

            def v(which, m):
                return vec[:, 2 * which + m:2 * which + m + 1]

            p_ctx = ExitStack()
            with p_ctx:
                stage_a = sb("stage_a", [P, KD, MATS_A * L], F32, p_ctx)
                stage_q = sb("stage_q", [P, KD, 3 * D], F32, p_ctx)
                stage_g = sb("stage_g", [P, KD, E], F32, p_ctx)
                p_wa, p_q, p_g, p_v, p_b, p_id, p_act, p_vec, p_self, p_hi = (
                    sem(n) for n in ("p_wa", "p_q", "p_g", "p_v", "p_b", "p_id", "p_act", "p_vec", "p_self", "p_hi"))
                with nc.Block() as block:
                    @block.sync
                    def _(sp):
                        sp.dma_start(vec[:, :], vecs).then_inc(p_v, 16)
                        for kk in range(KD):
                            sp.dma_start(stage_a[:, kk, :], mats_a[kk * P:(kk + 1) * P, :]).then_inc(p_wa, 16)
                        for kk in range(KD):
                            sp.dma_start(stage_q[:, kk, :], w_qkv[kk * P:(kk + 1) * P, :]).then_inc(p_q, 16)
                        for kk in range(KD):
                            sp.dma_start(stage_g[:, kk, :], gate_w[kk * P:(kk + 1) * P, :]).then_inc(p_g, 16)
                        sp.dma_start(boutb[:, :], b_out.rearrange("(o d) -> o d", o=1).broadcast_to([P, D])).then_inc(p_b, 16)
                        sp.dma_start(taub[:, :], tau.rearrange("(o d) -> o d", o=1).broadcast_to([P, 1])).then_inc(p_b, 16)
                        sp.dma_start(nub[:, :], nu.rearrange("(o d) -> o d", o=1).broadcast_to([P, 1])).then_inc(p_b, 16)
                        sp.wait_ge(p_b, 48)

                    @block.gpsimd
                    def _(pool):
                        pool.memset(ident[:, :], 0.0).then_inc(p_id, 1)
                        pool.memset(maskb[:, :], 0.0).then_inc(p_id, 1)
                        pool.memset(mhalf[:, :], -0.5).then_inc(p_id, 1)
                        pool.memset(phalf[:, :], 0.5).then_inc(p_id, 1)
                        pool.memset(one[:, :], 1.0).then_inc(p_id, 1)
                        pool.wait_ge(p_id, 5)
                        pool.affine_select(out=ident[:, :], in_=ident[:, :], compare_op=ALU.not_equal, fill=1.0,
                                           base=0, pattern=[[-1, P]], channel_multiplier=1).then_inc(p_id, 1)
                        pool.affine_select(out=maskb[:, :], in_=maskb[:, :], compare_op=ALU.is_ge, fill=NEG,
                                           base=0, pattern=[[-1, P]], channel_multiplier=1).then_inc(p_id, 1)
                        pool.wait_ge(p_id, 7)
                        pool.tensor_copy(identb[:, :], ident[:, :]).then_inc(p_id, 1)
                        pool.wait_ge(p_hi, 2)
                        pool.tensor_tensor(wqkv[1][:, :, :], stage_q[:, :, :], wqkv[0][:, :, :].bitcast(F32),
                                           ALU.subtract).then_inc(p_id, 1)
                        pool.tensor_tensor(gw[1][:, :, :], stage_g[:, :, :], gw[0][:, :, :].bitcast(F32),
                                           ALU.subtract).then_inc(p_id, 1)

                    @block.scalar
                    def _(act):
                        act.wait_ge(p_v, 16)
                        act.activation(sp1[:, :], vec[:, 2 * V_AP:2 * V_AP + 2], ACT.Abs).then_inc(p_act, 1)
                        act.wait_ge(p_act, 1)
                        act.activation(sp2[:, :], sp1[:, :], ACT.Exp, scale=-1.0).then_inc(p_act, 1)
                        act.wait_ge(p_act, 2)
                        act.wait_ge(p_id, 5)
                        act.activation(sp1[:, :], sp2[:, :], ACT.Ln, bias=one[:, :]).then_inc(p_act, 1)
                        act.wait_ge(p_q, 16 * KD)
                        act.activation(wqkv[0][:, :, :], stage_q[:, :, :], ACT.Copy).then_inc(p_hi, 1)
                        act.wait_ge(p_g, 16 * KD)
                        act.activation(gw[0][:, :, :], stage_g[:, :, :], ACT.Copy).then_inc(p_hi, 1)

                    @block.vector
                    def _(dve):
                        for kk in range(KD):
                            dve.wait_ge(p_wa, 16 * KD)
                            dve.tensor_copy(wa[0][:, kk, :], stage_a[:, kk, :]).then_inc(p_self, 1)
                            dve.wait_ge(p_self, 2 * kk + 1)
                            dve.tensor_tensor(wa[1][:, kk, :], stage_a[:, kk, :], wa[0][:, kk, :].bitcast(F32),
                                              ALU.subtract).then_inc(p_self, 1)
                        dve.wait_ge(p_act, 3)
                        dve.scalar_tensor_tensor(out=nsp[:, :], in0=vec[:, 2 * V_AP:2 * V_AP + 2], scalar=0.0,
                                                 in1=sp1[:, :], op0=ALU.max, op1=ALU.add).then_inc(p_self, 1)
                        dve.wait_ge(p_self, 2 * KD + 1)
                        dve.tensor_scalar(nsp[:, :], nsp[:, :], -8.0, None, ALU.mult).then_inc(p_self, 1)
                clear_all()

            xs = sba("xs_a", [P, TT, D])
            xn = sba("xn_a", [P, TT, D])
            st1 = sba("st1", [P, KD, W1Q])
            st2 = sba("st2", [P, W2Q, D])
            xb = sba("xb", [P, 2, TAPS - 1 + T])
            cv = sba("cv", [P, 2, T])
            sh = sba("sh", [P, 2, T], F32R)
            sl = sba("sl", [P, 2, T], F32R)
            gx = sba("gx", [P, 2, T])
            av = sba("av", [P, 2, T])
            yv = sba("yv", [P, 2, T])

            (a_x, a_w1, a_w2, a_out, a_ln, a_rstd, a_xn, a_tp, a_hi, a_lo, a_ps, a_xb, a_y, a_conv, a_chi, a_clo,
             a_gate, a_g, a_e, a_na, a_m, a_hy, a_hyh, a_hyl, a_o, a_xr, a_wh, a_wl, a_self, a_pool, a_xsum,
             a_tfree) = (
                sem(n) for n in (
                    "a_x", "a_w1", "a_w2", "a_out", "a_ln", "a_rstd", "a_xn", "a_tp", "a_hi", "a_lo", "a_ps", "a_xb",
                    "a_y", "a_conv", "a_chi", "a_clo", "a_gate", "a_g", "a_e", "a_na", "a_m", "a_hy", "a_hyh",
                    "a_hyl", "a_o", "a_xr", "a_wh", "a_wl", "a_self", "a_pool", "a_xsum", "a_tfree"))

            bT, bXB, bG, bY = (0, 1), (2, 3), (4, 5, 6, 7), (0, 1)
            with nc.Fori(0, B) as it:
                with nc.Block() as block:
                    @block.sync
                    def _(sp):
                        sp.dma_start(xs[:, :, :], x_rows[bass.ds(it, 1), :, :, :].rearrange("o p t d -> (o p) t d")).then_inc(a_x, 16)
                        for kk in range(KD):
                            sp.dma_start(st1[:, kk, :], w1[kk * P:(kk + 1) * P, bass.ds(it * W1Q, W1Q)]).then_inc(a_w1, 16)
                        sp.dma_start(st2[:, :, :], w2.rearrange("(q c p) d -> q p c d", p=P, q=QA)[bass.ds(it, 1), :, :, :]
                                     .rearrange("o p c d -> (o p) c d")).then_inc(a_w2, 16)
                        sp.wait_ge(a_xsum, TT)
                        sp.dma_start(out_rows[bass.ds(it, 1), :, :, :].rearrange("o p t d -> (o p) t d"), xs[:, :, :]).then_inc(a_out, 16)
                        sp.wait_ge(a_out, 16)

                    @block.gpsimd
                    def _(pool):
                        pool.wait_ge(a_ln, TT)
                        pool.tensor_scalar(vare[:, :], mv[:, :, 1], LN_EPS, None, ALU.add).then_inc(a_pool, 1)
                        pool.wait_ge(a_pool, 1)
                        pool.tensor_tensor(rstd[:, :], vare[:, :], mhalf[:, :], ALU.pow).then_inc(a_rstd, 1)
                        pool.wait_ge(a_xn, TT)
                        for t in range(TT):
                            pool.tensor_tensor(xs[:, t, :], xs[:, t, :], boutb[:, :], ALU.add).then_inc(a_xr, 1)
                        pool.wait_ge(a_wh, 1)
                        pool.tensor_tensor(w1l[:, :, bass.ds(it * W1Q, W1Q)], st1[:, :, :],
                                           w1h[:, :, bass.ds(it * W1Q, W1Q)].bitcast(F32), ALU.subtract).then_inc(a_wl, 1)
                        pool.wait_ge(a_wh, 2)
                        pool.tensor_tensor(w2l[:, bass.ds(it * W2Q, W2Q), :], st2[:, :, :],
                                           w2h[:, bass.ds(it * W2Q, W2Q), :].bitcast(F32), ALU.subtract).then_inc(a_wl, 1)

                    @block.scalar
                    def _(act):
                        for kk in range(KD):
                            act.wait_ge(a_tp, kk + 1)
                            act.activation(xTh[0][:, kk, :], banks[bT[kk]][:, :], ACT.Copy).then_inc(a_hi, 1)
                        for m in range(2):
                            act.wait_ge(a_ps, m + 1)
                            act.activation(xb[:, m, TAPS - 1:], banks[bXB[m]][:, :], ACT.Identity, bias=v(V_BX, m)).then_inc(a_xb, 1)
                        for m in range(2):
                            act.wait_ge(a_ps, m + 3)
                            act.activation(yv[:, m, :], banks[bY[m]][:, :], ACT.Gelu, bias=v(V_BY, m)).then_inc(a_y, 1)
                        for m in range(2):
                            act.wait_ge(a_conv, m + 1)
                            act.activation(sh[:, m, :], cv[:, m, :], ACT.Copy).then_inc(a_chi, 1)
                        act.wait_ge(a_w1, 16 * KD)
                        act.activation(w1h[:, :, bass.ds(it * W1Q, W1Q)], st1[:, :, :], ACT.Copy).then_inc(a_wh, 1)
                        for j in range(4):
                            dst, b = ((gx, V_BIG), (av, V_BAG))[j // 2]
                            act.wait_ge(a_gate, j + 1)
                            act.activation(dst[:, j % 2, :], banks[bG[j]][:, :], ACT.Sigmoid, bias=v(b, j % 2)).then_inc(a_g, 1)
                        act.wait_ge(a_g, 4)
                        for m in range(2):
                            act.activation(av[:, m, :], av[:, m, :], ACT.Exp, scale=nsp[:, m:m + 1]).then_inc(a_e, 1)
                        for m in range(2):
                            act.wait_ge(a_na, m + 1)
                            act.activation(xb[:, m, TAPS - 1:], xb[:, m, TAPS - 1:], ACT.Sqrt, bias=one[:, :]).then_inc(a_m, 1)
                        act.wait_ge(a_w2, 16)
                        act.activation(w2h[:, bass.ds(it * W2Q, W2Q), :], st2[:, :, :], ACT.Copy).then_inc(a_wh, 1)
                        for m in range(2):
                            act.wait_ge(a_hy, m + 1)
                            act.activation(sh[:, m, :], yv[:, m, :], ACT.Copy).then_inc(a_hyh, 1)

                    @block.vector
                    def _(dve):
                        n = Count()

                        def link(ins):
                            ins.then_inc(a_self, 1)
                            dve.wait_ge(a_self, n.next("self"))

                        dve.memset(xb[:, :, 0:TAPS - 1], 0.0).then_inc(a_self, 1)
                        n.next("self")
                        dve.wait_ge(a_x, 16)
                        for t in range(TT):
                            link(dve.bn_stats(stats[:, t, :], xs[:, t, :]))
                            dve.bn_aggr(mv[:, t, :], stats[:, t, :]).then_inc(a_ln, 1)
                        dve.wait_ge(a_rstd, 1)
                        for t in range(TT):
                            dve.tensor_scalar(xn[:, t, :], xs[:, t, :], mv[:, t, 0:1], rstd[:, t:t + 1],
                                              ALU.subtract, ALU.mult).then_inc(a_xn, 1)
                        for kk in range(KD):
                            dve.wait_ge(a_hi, kk + 1)
                            dve.tensor_tensor(xTl[0][:, kk, :], banks[bT[kk]][:, :], xTh[0][:, kk, :].bitcast(F32),
                                              ALU.subtract).then_inc(a_lo, 1)
                        for m in range(2):
                            dve.wait_ge(a_xb, m + 1)
                            link(dve.tensor_scalar(cv[:, m, :], xb[:, m, TAPS - 1:], v(V_CW + TAPS - 1, m), v(V_CB, m),
                                                   ALU.mult, ALU.add))
                            for k in range(TAPS - 1):
                                last = dve.scalar_tensor_tensor(out=cv[:, m, :], in0=xb[:, m, k:k + T], scalar=v(V_CW + k, m),
                                                                in1=cv[:, m, :], op0=ALU.mult, op1=ALU.add)
                                if k < TAPS - 2:
                                    link(last)
                            last.then_inc(a_conv, 1)
                            dve.wait_ge(a_chi, m + 1)
                            dve.tensor_tensor(sl[:, m, :], cv[:, m, :], sh[:, m, :].bitcast(F32), ALU.subtract).then_inc(a_clo, 1)
                        for m in range(2):
                            dve.wait_ge(a_g, m + 1)
                            link(dve.tensor_tensor(gx[:, m, :], gx[:, m, :], cv[:, m, :], ALU.mult))
                        for m in range(2):
                            dve.wait_ge(a_e, m + 1)
                            link(dve.memset(av[:, m, 0:1], 0.0))
                            dve.scalar_tensor_tensor(out=xb[:, m, TAPS - 1:], in0=av[:, m, :], scalar=-1.0,
                                                     in1=av[:, m, :], op0=ALU.mult, op1=ALU.mult).then_inc(a_na, 1)
                        for m in range(2):
                            dve.wait_ge(a_m, m + 1)
                            link(dve.tensor_tensor(gx[:, m, :], gx[:, m, :], xb[:, m, TAPS - 1:], ALU.mult))
                            link(dve.tensor_tensor_scan(cv[:, m, :], av[:, m, :], gx[:, m, :], 0.0, ALU.mult, ALU.add))
                            dve.wait_ge(a_y, m + 1)
                            dve.tensor_tensor(yv[:, m, :], cv[:, m, :], yv[:, m, :], ALU.mult).then_inc(a_hy, 1)
                            dve.wait_ge(a_hyh, m + 1)
                            dve.tensor_tensor(sl[:, m, :], yv[:, m, :], sh[:, m, :].bitcast(F32), ALU.subtract).then_inc(a_hyl, 1)
                        for t in range(TT):
                            dve.wait_ge(a_xr, t + 1)
                            dve.wait_ge(a_o, t + 1)
                            dve.tensor_tensor(xs[:, t, :], banks[bG[t]][:, 0:D], xs[:, t, :], ALU.add).then_inc(a_xsum, 1)

                    @block.tensor
                    def _(pe):
                        pe.wait_ge(a_xn, TT)
                        for kk in range(KD):
                            for t in range(TT):
                                last = pe.transpose(banks[bT[kk]][:, t * P:(t + 1) * P], xn[:, t, kk * P:(kk + 1) * P], ident[:, :])
                            last.then_inc(a_tp, 1)

                        def product(bank, mat, m, hi, lo):
                            for kk in range(KD):
                                w = [wa[i][:, kk, mat * L + m * P:mat * L + (m + 1) * P] for i in range(2)]
                                pe.matmul(bank, w[0], hi[:, kk, :], start=(kk == 0), stop=False)
                                pe.matmul(bank, w[1], hi[:, kk, :], start=False, stop=False)
                                last = pe.matmul(bank, w[0], lo[:, kk, :], start=False, stop=(kk == KD - 1))
                            return last

                        pe.wait_ge(a_hi, KD)
                        pe.wait_ge(a_lo, KD)
                        for m in range(2):
                            product(banks[bXB[m]][:, :], M_X, m, xTh[0], xTl[0]).then_inc(a_ps, 1)
                        for m in range(2):
                            product(banks[bY[m]][:, :], M_Y, m, xTh[0], xTl[0]).then_inc(a_ps, 1)
                        pe.wait_ge(a_chi, 2)
                        pe.wait_ge(a_clo, 2)
                        for j in range(4):
                            product(banks[bG[j]][:, :], (M_IG, M_AG)[j // 2], j % 2, sh, sl).then_inc(a_gate, 1)
                        pe.wait_ge(a_hyh, 2)
                        pe.wait_ge(a_hyl, 2)
                        for t in range(TT):
                            for kk in range(KD):
                                w = [wa[i][:, kk, M_OUT * L:(M_OUT + 1) * L] for i in range(2)]
                                tok = slice(t * P, (t + 1) * P)
                                pe.matmul(banks[bG[t]][:, 0:D], sh[:, kk, tok], w[0], start=(kk == 0), stop=False)
                                pe.matmul(banks[bG[t]][:, 0:D], sh[:, kk, tok], w[1], start=False, stop=False)
                                last = pe.matmul(banks[bG[t]][:, 0:D], sl[:, kk, tok], w[0], start=False, stop=(kk == KD - 1))
                            last.then_inc(a_o, 1)
                clear_all()

        Z, CWB, ACC, SC, TP, OV = banks[0], banks[1], banks[2:4], banks[4:6], banks[6], banks[7]

        xs = sb("xs", [P, PAIR, TT, D])
        big = sb("big", [P, TT * D])
        xn = big[:, :].rearrange("p (t d) -> p t d", t=TT)
        yT = big[:, :].rearrange("p (m t) -> p m t", m=KD)
        th = sb("th", [P, 2, T])
        tv = sb("tv", [P, 2, T])
        tvh = sb("tvh", [P, 2, T], F32R)
        tvl = sb("tvl", [P, 2, T], F32R)
        cT = [sb(f"cT{b}", [P, T], F32R) for b in range(PAIR)]
        score = sb("score", [P, TT, G, GS])
        pmx = sb("pmx", [P, TT, G, 2])
        pmn = sb("pmn", [P, TT, G, 2])
        gsum = sb("gsum", [P, TT, G])
        gbest = sb("gbest", [P, TT, G])
        gcmp = sb("gcmp", [P, TT, G, G])
        gcm2 = sb("gcm2", [P, TT, G, G])
        tri = sb("tri", [P, G, G])
        iot = sb("iot", [P, E])
        top8 = sb("top8", [P, TT, 8])
        idx8 = sb("idx8", [P, TT, 8], U32)
        idxf = sb("idxf", [P, TT, TOPK])
        wsum = sb("wsum", [P, TT])
        wtop = sb("wtop", [P, TT, TOPK])
        cw = sb("cw", [P, TT, E])
        cw2 = sb("cw2", [P, TT, E])
        cc = sb("cc", [P, TT, P], F32R)
        sq = sb("sq", [P, 2, 3 * HW])
        nrm = sb("nrm", [P, 3 * HH])
        nrt = sb("nrt", [P, 3 * HH])
        qkn = sb("qkn", [P, 2 * HW])
        stq = sb("stq", [P, HH, 4, HD], F32R)
        stk = sb("stk", [P, HH, 4, HD], F32R)
        qT = sb("qT", [P, HP, T], F32R)
        kT = sb("kT", [P, HP, T], F32R)
        vt = sb("vt", [P, TT, HW])
        pr = sb("pr", [P, 2, T])
        prT = sb("prT", [P, 2, T])
        nmax = sb("nmax", [P, 2])
        den = sb("den", [P, 2, HH])
        rden = sb("rden", [P, HH])
        ov = sb("ov", [P, HW])

        UNITS = [(qt, h) for qt in range(TT) for h in range(HH)]
        NU = len(UNITS)
        N_EXPERTS = 3 * (NCH + 1)
        N_LN, N_ROUTE, N_FIN = 6, 8, 4
        N_HALF = TT + 2 + NU + 4
        X_EXPERTS, X_ATTENTION = 2, 2 * TT

        def evacuates(u):
            return "dve" if u % 3 == 2 else "act"

        (x_in, x_out, c_sel, c_pool, self_dve, self_pool, ln_stats, rstd_ok, xn_ok, xt_ps, xt_hi, xt_lo, rt_ps,
         rt_exp, comb_ok, ct_ps, ct_ok, z_full, tanh_ok, z_used, c_full, t_ok, th_ok, tl_ok, o_done, acc_out,
         fin_ps, x_upd, qkv_ps, sq_ok, nrm_ok, nrt_ok, qkv_used, qk_ok, sh_ok, st_ok, stT_ps, qkT_ok, sc_ps,
         max_ok, p_ok, pT_ps, pT_ok, pv_ps, ov_free) = (
            sem(name) for name in (
                "x_in", "x_out", "c_sel", "c_pool", "self_dve", "self_pool", "ln_stats", "rstd_ok", "xn_ok",
                "xt_ps", "xt_hi", "xt_lo", "rt_ps", "rt_exp", "comb_ok", "ct_ps", "ct_ok", "z_full", "tanh_ok",
                "z_used", "c_full", "t_ok", "th_ok", "tl_ok", "o_done", "acc_out", "fin_ps", "x_upd", "qkv_ps",
                "sq_ok", "nrm_ok", "nrt_ok", "qkv_used", "qk_ok", "sh_ok", "st_ok", "stT_ps", "qkT_ok", "sc_ps",
                "max_ok", "p_ok", "pT_ps", "pT_ok", "pv_ps", "ov_free"))

        SELC = NROUTED * P // 4
        assert SELC <= TT * D
        with nc.Block() as block:
            @block.gpsimd
            def _(pool):
                pool.memset(tri[:, :, :], 1.0).then_inc(c_pool, 1)
                pool.memset(cc[:, :, :].bitcast(F32), 0.0).then_inc(c_pool, 1)
                pool.iota(iot[:, :], pattern=[[1, E]], base=0, channel_multiplier=0,
                          allow_small_or_imprecise_dtypes=True).then_inc(c_pool, 1)
                pool.wait_ge(c_pool, 3)
                pool.affine_select(out=tri[:, :, :], in_=tri[:, :, :], compare_op=ALU.is_gt, fill=0.0,
                                   base=0, pattern=[[1, G], [-1, G]], channel_multiplier=0).then_inc(c_pool, 1)

            @block.sync
            def _(sp):
                for j in range(4):
                    sp.wait_ge(c_sel, j + 1)
                    sp.dma_start(big[0:2 * E, 0:SELC], sel[:, j * SELC:(j + 1) * SELC]).then_inc(x_in, 16)

            @block.vector
            def _(dve):
                dve.memset(big[:, :], 0.0).then_inc(c_sel, 1)
                for j in range(4):
                    dve.wait_ge(x_in, 16 * (j + 1))
                    dve.tensor_copy(selr[:, j * SELC:(j + 1) * SELC], big[:, 0:SELC]).then_inc(c_sel, 1)
        clear_all()

        def round_of_two(norm, route, experts, finish, half):
            def attention(b):
                yield from finish(b)
                yield from norm(b)
                yield from half(b, 0)
                yield from half(b, 1)
                yield from norm(b)
                yield from route(b)

            def norm_route(b):
                yield from norm(b)
                yield from route(b)

            n_attention = N_FIN + 2 * N_LN + 2 * N_HALF + N_ROUTE
            for _ in norm_route(0):
                pass
            weave(experts(0), N_EXPERTS, norm_route(1), N_LN + N_ROUTE)
            weave(experts(1), N_EXPERTS, attention(0), n_attention)
            weave(experts(0), N_EXPERTS, attention(1), n_attention)
            weave(experts(1), N_EXPERTS, finish(0), N_FIN)
            for _ in finish(1):
                pass

        with nc.Fori(0, B // PAIR) as it:
            with nc.Block() as block:
                @block.sync
                def _(sp):
                    for b in range(PAIR):
                        sp.dma_start(xs[:, b, :, :], out_rows[bass.ds(it * PAIR + b, 1), :, :, :]
                                     .rearrange("o p t d -> (o p) t d")).then_inc(x_in, 16)
                    for b in range(PAIR):
                        sp.wait_ge(x_upd, PAIR * (X_EXPERTS + X_ATTENTION) + (b + 1) * X_EXPERTS)
                        sp.dma_start(out_rows[bass.ds(it * PAIR + b, 1), :, :, :].rearrange("o p t d -> (o p) t d"),
                                     xs[:, b, :, :]).then_inc(x_out, 16)
                    sp.wait_ge(x_out, 16 * PAIR)

                @block.tensor
                def _(pe):
                    n = Count()

                    def split_product(o, a, b, start, stop):
                        pe.matmul(o, a[0], b[0], start=start, stop=False)
                        pe.matmul(o, a[1], b[0], start=False, stop=False)
                        return pe.matmul(o, a[0], b[1], start=False, stop=stop)

                    def norm(b):
                        for _ in range(3):
                            yield
                        pe.wait_ge(xn_ok, n.next("xn", TT))
                        for kk in range(KD):
                            for t in range(TT):
                                last = pe.transpose(SC[kk][:, t * P:(t + 1) * P], xn[:, t, kk * P:(kk + 1) * P], ident[:, :])
                            last.then_inc(xt_ps, 1)
                            yield
                        pe.wait_ge(xt_lo, n.next("xt_lo", KD))
                        yield

                    def route(b):
                        for t in range(TT):
                            tok = slice(t * P, (t + 1) * P)
                            for kk in range(KD):
                                last = split_product(TP[:, t * E:(t + 1) * E], (xTh[b][:, kk, tok], xTl[b][:, kk, tok]),
                                                     (gw[0][:, kk, :], gw[1][:, kk, :]), kk == 0, kk == KD - 1)
                        last.then_inc(rt_ps, 1)
                        for _ in range(N_ROUTE - 2):
                            yield
                        pe.wait_ge(comb_ok, n.next("comb"))
                        for t in range(TT):
                            last = pe.transpose(TP[:, t * P:(t + 1) * P], cc[:, t, :].bitcast(F32), ident[:, :])
                        last.then_inc(ct_ps, 1)
                        yield
                        yield

                    def experts(b):
                        pe.wait_ge(ct_ok, n.next("ct"))
                        inst = n.before("experts")
                        for c in range(NCH + 1):
                            g = inst * NCH + c
                            if c < NCH:
                                hid = slice(c * P, (c + 1) * P)
                                if g:
                                    pe.wait_ge(z_used, g)
                                for kk in range(KD):
                                    last = split_product(Z[:, :], (w1h[:, kk, hid], w1l[:, kk, hid]),
                                                         (xTh[b][:, kk, :], xTl[b][:, kk, :]), kk == 0, kk == KD - 1)
                                last.then_inc(z_full, 1)
                            if c < NROUTED:
                                if g:
                                    pe.wait_ge(t_ok, g)
                                pe.matmul(CWB[:, :], selr[:, c * P:(c + 1) * P], cT[b][:, :], start=True, stop=True).then_inc(c_full, 1)
                            yield
                            if c >= 1:
                                if c == 1 and inst:
                                    pe.wait_ge(acc_out, KD * inst)
                                pe.wait_ge(th_ok, g)
                                pe.wait_ge(tl_ok, g)
                            for m in range(KD):
                                if c >= 1:
                                    k = (g - 1) % 2
                                    last = split_product(ACC[m][:, :], (w2h[:, c - 1, m * P:(m + 1) * P], w2l[:, c - 1, m * P:(m + 1) * P]),
                                                         (tvh[:, k, :], tvl[:, k, :]), c == 1, c == NCH)
                                    if m == KD - 1:
                                        last.then_inc(o_done, 1)
                                yield

                    def finish(b):
                        yield
                        pe.wait_ge(acc_out, n.next("acc", KD))
                        for j in range(2):
                            for t in range(2):
                                for kk in range(KD):
                                    last = pe.transpose(SC[j][:, t * D + kk * P:t * D + (kk + 1) * P],
                                                        yT[:, kk, (2 * j + t) * P:(2 * j + t + 1) * P], ident[:, :])
                            last.then_inc(fin_ps, 1)
                            yield
                        yield

                    def half(b, hf):
                        cols = slice(hf * 3 * HW, (hf + 1) * 3 * HW)
                        for t in range(TT + 2):
                            if t < TT:
                                if t >= 2:
                                    pe.wait_ge(qkv_used, n.n.get("qkv_used", 0) + t - 1)
                                tok = slice(t * P, (t + 1) * P)
                                for kk in range(KD):
                                    last = split_product(SC[t % 2][:, 0:3 * HW], (xTh[b][:, kk, tok], xTl[b][:, kk, tok]),
                                                         (wqkv[0][:, kk, cols], wqkv[1][:, kk, cols]), kk == 0, kk == KD - 1)
                                last.then_inc(qkv_ps, 1)
                            if t >= 2:
                                pe.wait_ge(st_ok, n.next("st", 2))
                                k = n.n.get("qkT", 0) + 2 * (t - 2)
                                if k:
                                    pe.wait_ge(qkT_ok, k)
                                for bank, st in ((TP, stq), (OV, stk)):
                                    rows = st[:, :, :, :].bitcast(F32).rearrange("p (j h) f d -> p j (h f d)", h=2)
                                    if bank is OV and t == 2 and n.n.get("ov", 0):
                                        pe.wait_ge(ov_free, n.n["ov"])
                                    for j in range(HP):
                                        last = pe.transpose(bank[:, j * P:(j + 1) * P], rows[:, j, :], ident[:, :])
                                    last.then_inc(stT_ps, 1)
                            yield
                        n.next("qkv_used", TT)
                        pe.wait_ge(qkT_ok, n.next("qkT", 2 * TT))
                        for u in range(NU + 4):
                            if 3 <= u < NU + 3:
                                qt, h = UNITS[u - 3]
                                pe.wait_ge(pT_ok, n.next("pT"))
                                if h == 0 and n.before("ov"):
                                    pe.wait_ge(ov_free, n.n["ov"] - 1)
                                for j in range(qt + 1):
                                    last = pe.matmul(OV[:, h * HD:(h + 1) * HD], prT[:, (u - 3) % 2, j * P:(j + 1) * P],
                                                     vt[:, j, h * HD:(h + 1) * HD], start=(j == 0), stop=(j == qt))
                                last.then_inc(pv_ps, 1)
                            if 2 <= u < NU + 2:
                                qt, h = UNITS[u - 2]
                                pe.wait_ge(p_ok, n.next("p"))
                                for j in range(qt + 1):
                                    last = pe.transpose(TP[:, j * P:(j + 1) * P], pr[:, u % 2, j * P:(j + 1) * P], ident[:, :])
                                last.then_inc(pT_ps, 1)
                            if u < NU:
                                qt, h = UNITS[u]
                                w = (qt + 1) * P
                                r = slice((h % 2) * 64, (h % 2) * 64 + 64)
                                pe.matmul(SC[u % 2][:, 0:w], qT[r, h // 2, qt * P:(qt + 1) * P], kT[r, h // 2, 0:w],
                                          start=True, stop=False)
                                pe.matmul(SC[u % 2][:, w - P:w], identb[:, :], maskb[:, :], start=False, stop=True).then_inc(sc_ps, 1)
                            yield

                    round_of_two(norm, route, experts, finish, half)

                @block.scalar
                def _(act):
                    n = Count()

                    def norm(b):
                        for _ in range(3):
                            yield
                        for kk in range(KD):
                            act.wait_ge(xt_ps, n.next("xt"))
                            act.activation(xTh[b][:, kk, :], SC[kk][:, :], ACT.Copy).then_inc(xt_hi, 1)
                            yield
                        yield

                    def route(b):
                        act.wait_ge(rt_ps, n.next("rt"))
                        act.activation(score[:, :, :, :].rearrange("p t g e -> p (t g e)"), TP[:, 0:TT * E], ACT.Exp,
                                       scale=-1.0).then_inc(rt_exp, 1)
                        for _ in range(N_ROUTE - 2):
                            yield
                        act.wait_ge(ct_ps, n.next("ct"))
                        act.activation(cT[b][:, :], TP[:, :], ACT.Copy).then_inc(ct_ok, 1)
                        yield
                        yield

                    def experts(b):
                        for c in range(NCH + 1):
                            if c < NCH:
                                g = n.before("z")
                                act.wait_ge(z_full, g + 1)
                                if g >= 2:
                                    act.wait_ge(t_ok, g - 1)
                                act.activation(th[:, g % 2, :], Z[:, :], ACT.Tanh, scale=0.5).then_inc(tanh_ok, 1)
                            yield
                            yield
                            yield

                    def finish(b):
                        act.wait_ge(o_done, n.next("fin", NCH))
                        act.activation(yT[:, 0, :], ACC[0][:, :], ACT.Copy).then_inc(acc_out, 1)
                        for _ in range(N_FIN):
                            yield

                    def half(b, hf):
                        for t in range(TT + 2):
                            if t < TT:
                                act.wait_ge(qkv_ps, n.next("qkv"))
                                act.activation(sq[:, t % 2, :], SC[t % 2][:, 0:3 * HW], ACT.Square).then_inc(sq_ok, 1)
                            if t >= 2:
                                for bank, dst in ((TP, qT), (OV, kT)):
                                    act.wait_ge(stT_ps, n.next("stT"))
                                    act.activation(dst[:, :, (t - 2) * P:(t - 1) * P],
                                                   bank[:, :].rearrange("p (j q) -> p j q", j=HP), ACT.Copy).then_inc(qkT_ok, 1)
                            yield
                        for u in range(NU + 4):
                            if u < NU:
                                qt, h = UNITS[u]
                                w = (qt + 1) * P
                                act.wait_ge(max_ok, n.next("max"))
                                act.activation(pr[:, u % 2, 0:w], SC[u % 2][:, 0:w], ACT.Exp, bias=nmax[:, u % 2:u % 2 + 1],
                                               accum_out=den[:, qt % 2, h:h + 1]).then_inc(p_ok, 1)
                            if 2 <= u < NU + 2:
                                qt, h = UNITS[u - 2]
                                k = n.next("pT")
                                if evacuates(u - 2) == "act":
                                    act.wait_ge(pT_ps, k)
                                    act.activation(prT[:, u % 2, 0:(qt + 1) * P], TP[:, 0:(qt + 1) * P], ACT.Copy).then_inc(pT_ok, 1)
                            yield

                    round_of_two(norm, route, experts, finish, half)

                @block.gpsimd
                def _(pool):
                    n = Count()

                    def norm(b):
                        pool.wait_ge(ln_stats, n.next("ln", TT))
                        pool.tensor_scalar(vare[:, :], mv[:, :, 1], LN_EPS, None, ALU.add).then_inc(self_pool, 1)
                        pool.wait_ge(self_pool, n.next("self"))
                        pool.tensor_tensor(rstd[:, :], vare[:, :], mhalf[:, :], ALU.pow).then_inc(rstd_ok, 1)
                        for _ in range(N_LN):
                            yield

                    def route(b):
                        for _ in range(N_ROUTE):
                            yield

                    def experts(b):
                        for c in range(NCH + 1):
                            if c < NCH:
                                g = n.before("t")
                                pool.wait_ge(t_ok, g + 1)
                                if g >= 2:
                                    pool.wait_ge(o_done, g - 1)
                                pool.tensor_copy(tvh[:, g % 2, :], tv[:, g % 2, :]).then_inc(th_ok, 1)
                                pool.wait_ge(th_ok, g + 1)
                                pool.tensor_tensor(tvl[:, g % 2, :], tv[:, g % 2, :], tvh[:, g % 2, :].bitcast(F32),
                                                   ALU.subtract).then_inc(tl_ok, 1)
                            yield
                            yield
                            yield

                    def finish(b):
                        for _ in range(N_FIN):
                            yield

                    def half(b, hf):
                        for t in range(TT + 2):
                            if t < TT:
                                pool.wait_ge(nrm_ok, n.next("nrm"))
                                pool.tensor_tensor(nrt[:, :], nrm[:, :], phalf[:, :], ALU.pow).then_inc(nrt_ok, 1)
                            yield
                        for u in range(NU + 4):
                            yield

                    round_of_two(norm, route, experts, finish, half)

                @block.vector
                def _(dve):
                    n = Count()

                    def link(ins):
                        ins.then_inc(self_dve, 1)
                        dve.wait_ge(self_dve, n.next("self"))

                    def norm(b):
                        if n.n.get("upd", 0):
                            dve.wait_ge(x_upd, n.n["upd"])
                        else:
                            dve.wait_ge(x_in, 16 * PAIR)
                        for t in range(TT):
                            link(dve.bn_stats(stats[:, t, :], xs[:, b, t, :]))
                            dve.bn_aggr(mv[:, t, :], stats[:, t, :]).then_inc(ln_stats, 1)
                        yield
                        dve.wait_ge(rstd_ok, n.next("rstd"))
                        for t in range(TT):
                            dve.tensor_scalar(xn[:, t, :], xs[:, b, t, :], mv[:, t, 0:1], rstd[:, t:t + 1],
                                              ALU.subtract, ALU.mult).then_inc(xn_ok, 1)
                        yield
                        yield
                        for kk in range(KD):
                            dve.wait_ge(xt_hi, n.next("xt"))
                            dve.tensor_tensor(xTl[b][:, kk, :], SC[kk][:, :], xTh[b][:, kk, :].bitcast(F32),
                                              ALU.subtract).then_inc(xt_lo, 1)
                            yield
                        yield

                    def route(b):
                        flat = score[:, :, :, :].rearrange("p t g e -> p (t g e)")
                        dve.wait_ge(rt_exp, n.next("rt"))
                        link(dve.tensor_scalar(flat, flat, 1.0, None, ALU.add))
                        link(dve.reciprocal(flat, flat))
                        dve.tensor_tensor(pmx[:, :, :, :], score[:, :, :, 0:2], score[:, :, :, 2:4], ALU.max)
                        link(dve.tensor_tensor(pmn[:, :, :, :], score[:, :, :, 0:2], score[:, :, :, 2:4], ALU.min))
                        dve.tensor_tensor(gsum[:, :, :], pmx[:, :, :, 0], pmx[:, :, :, 1], ALU.max)
                        dve.tensor_tensor(gbest[:, :, :], pmx[:, :, :, 0], pmx[:, :, :, 1], ALU.min)
                        link(dve.tensor_tensor(pmn[:, :, :, 0], pmn[:, :, :, 0], pmn[:, :, :, 1], ALU.max))
                        link(dve.tensor_tensor(gbest[:, :, :], gbest[:, :, :], pmn[:, :, :, 0], ALU.max))
                        link(dve.tensor_tensor(gsum[:, :, :], gsum[:, :, :], gbest[:, :, :], ALU.add))
                        yield
                        shape = [P, TT, G, G]
                        other = gsum[:, :, :].unsqueeze(2).broadcast_to(shape)
                        own = gsum[:, :, :].unsqueeze(3).broadcast_to(shape)
                        dve.tensor_tensor(gcmp[:, :, :, :], other, own, ALU.is_gt)
                        link(dve.tensor_tensor(gcm2[:, :, :, :], other, own, ALU.is_ge))
                        link(dve.tensor_tensor(gcm2[:, :, :, :], gcm2[:, :, :, :],
                                               tri[:, :, :].unsqueeze(1).broadcast_to(shape), ALU.mult))
                        link(dve.tensor_tensor(gcmp[:, :, :, :], gcmp[:, :, :, :], gcm2[:, :, :, :], ALU.max))
                        link(dve.tensor_reduce(gbest[:, :, :], gcmp[:, :, :, :], AX_X, ALU.add))
                        link(dve.tensor_scalar(gbest[:, :, :], gbest[:, :, :], 2.0, None, ALU.is_lt))
                        link(dve.tensor_tensor(score[:, :, :, :], score[:, :, :, :],
                                               gbest[:, :, :].unsqueeze(3).broadcast_to([P, TT, G, GS]), ALU.mult))
                        yield
                        rows = score[:, :, :, :].rearrange("p t g e -> p t (g e)")
                        for t in range(TT):
                            link(dve.max(top8[:, t, :], rows[:, t, :]))
                        for t in range(TT):
                            last = dve.max_index(idx8[:, t, :], top8[:, t, :], rows[:, t, :])
                            if t == TT - 1:
                                link(last)
                        yield
                        dve.tensor_copy(idxf[:, :, :], idx8[:, :, 0:TOPK])
                        link(dve.tensor_tensor(wsum[:, :], top8[:, :, 0], top8[:, :, 1], ALU.add))
                        link(dve.tensor_scalar(wsum[:, :], wsum[:, :], TOP_EPS, None, ALU.add))
                        link(dve.reciprocal(wsum[:, :], wsum[:, :]))
                        link(dve.scalar_tensor_tensor(out=wtop[:, :, :], in0=top8[:, :, 0:TOPK], scalar=0.5,
                                                      in1=wsum[:, :].unsqueeze(2).broadcast_to([P, TT, TOPK]),
                                                      op0=ALU.mult, op1=ALU.mult))
                        yield
                        wide = [P, TT, E]
                        for j, c in enumerate((cw, cw2)):
                            link(dve.tensor_tensor(c[:, :, :], iot[:, :].unsqueeze(1).broadcast_to(wide),
                                                   idxf[:, :, j:j + 1].broadcast_to(wide), ALU.is_equal))
                            link(dve.tensor_tensor(c[:, :, :], c[:, :, :], wtop[:, :, j:j + 1].broadcast_to(wide), ALU.mult))
                        link(dve.tensor_tensor(cw[:, :, :], cw[:, :, :], cw2[:, :, :], ALU.add))
                        link(dve.tensor_copy(cc[:, :, 0:E], cw[:, :, :]))
                        dve.tensor_tensor(cc[:, :, E:2 * E], cw[:, :, :], cc[:, :, 0:E].bitcast(F32), ALU.subtract).then_inc(comb_ok, 1)
                        for _ in range(N_ROUTE - 4):
                            yield

                    def experts(b):
                        for c in range(NCH + 1):
                            if c < NCH:
                                g = n.before("z")
                                k = g % 2
                                dve.wait_ge(tanh_ok, g + 1)
                                dve.scalar_tensor_tensor(out=th[:, k, :], in0=th[:, k, :], scalar=1.0, in1=Z[:, :],
                                                         op0=ALU.add, op1=ALU.mult).then_inc(z_used, 1)
                                dve.wait_ge(z_used, g + 1)
                                if g >= 2:
                                    dve.wait_ge(tl_ok, g - 1)
                                if c < NROUTED:
                                    dve.wait_ge(c_full, n.next("c"))
                                    dve.tensor_tensor(tv[:, k, :], th[:, k, :], CWB[:, :], ALU.mult).then_inc(t_ok, 1)
                                else:
                                    dve.tensor_scalar(tv[:, k, :], th[:, k, :], 0.5, None, ALU.mult).then_inc(t_ok, 1)
                            yield
                            yield
                            yield

                    def finish(b):
                        dve.wait_ge(o_done, n.next("fin", NCH))
                        dve.tensor_copy(yT[:, 1, :], ACC[1][:, :]).then_inc(acc_out, 1)
                        yield
                        for j in range(2):
                            dve.wait_ge(fin_ps, n.next("fin_ps"))
                            rows = xs[:, b, 2 * j:2 * j + 2, :].rearrange("p t d -> p (t d)")
                            dve.tensor_tensor(rows, SC[j][:, :], rows, ALU.add).then_inc(x_upd, 1)
                            n.next("upd")
                            yield
                        yield

                    def half(b, hf):
                        for t in range(TT + 2):
                            if t < TT:
                                dve.wait_ge(sq_ok, n.next("sq"))
                                dve.tensor_reduce(nrm[:, :], sq[:, t % 2, :].rearrange("p (h d) -> p h d", d=HD),
                                                  AX_X, ALU.add).then_inc(nrm_ok, 1)
                                dve.wait_ge(nrt_ok, n.next("nrt"))
                                link(dve.tensor_scalar(nrt[:, :], nrt[:, :], L2_EPS, None, ALU.add))
                                link(dve.reciprocal(nrt[:, :], nrt[:, :]))
                                link(dve.tensor_scalar(nrt[:, 0:HH], nrt[:, 0:HH], taub[:, 0:1], None, ALU.mult))
                                src = SC[t % 2][:, 0:3 * HW].rearrange("p (h d) -> p h d", d=HD)
                                inv = nrt[:, :].unsqueeze(2).broadcast_to([P, 3 * HH, HD])
                                link(dve.tensor_tensor(qkn[:, :].rearrange("p (h d) -> p h d", d=HD),
                                                       src[:, 0:2 * HH, :], inv[:, 0:2 * HH, :], ALU.mult))
                                dve.tensor_tensor(vt[:, t, :].rearrange("p (h d) -> p h d", d=HD),
                                                  src[:, 2 * HH:, :], inv[:, 2 * HH:, :], ALU.mult).then_inc(qkv_used, 1)
                                k = n.n.get("stT", 0) + 2 * t
                                if k:
                                    dve.wait_ge(stT_ps, k)
                                for st, first, step, c in ((stq, (0, 1), 2, 0), (stk, (0, 2), 1, HW)):
                                    rows = qkn[:, c:c + HW].rearrange("p (h d) -> p h d", d=HD)
                                    both = rows.unsqueeze(2).broadcast_to([P, HH, 2, HD])
                                    hi = st[:, :, first[0]:first[0] + step + 1:step, :]
                                    lo = st[:, :, first[1]:first[1] + step + 1:step, :]
                                    link(dve.tensor_copy(hi, both))
                                    dve.tensor_tensor(lo, both, hi.bitcast(F32), ALU.subtract).then_inc(st_ok, 1)
                            yield
                        n.next("stT", 2 * TT)
                        for u in range(NU + 4):
                            if u < NU:
                                qt, h = UNITS[u]
                                dve.wait_ge(sc_ps, n.next("sc"))
                                dve.tensor_reduce(nmax[:, u % 2:u % 2 + 1], SC[u % 2][:, 0:(qt + 1) * P], AX_X, ALU.max,
                                                  negate=True).then_inc(max_ok, 1)
                            if 2 <= u < NU + 2:
                                qt, h = UNITS[u - 2]
                                k = n.next("pT")
                                if evacuates(u - 2) == "dve":
                                    dve.wait_ge(pT_ps, k)
                                    dve.tensor_copy(prT[:, u % 2, 0:(qt + 1) * P], TP[:, 0:(qt + 1) * P]).then_inc(pT_ok, 1)
                            if u >= 3:
                                k = n.n.get("pv", 0) + u - 2
                                if u < NU + 3 and UNITS[u - 3][1] == HH - 1:
                                    qt = UNITS[u - 3][0]
                                    dve.wait_ge(pv_ps, k)
                                    link(dve.reciprocal(rden[:, :], den[:, qt % 2, :]))
                                    link(dve.tensor_scalar(rden[:, :], rden[:, :], nub[:, 0:1], None, ALU.mult))
                                    dve.tensor_tensor(ov[:, :].rearrange("p (h d) -> p h d", d=HD),
                                                      OV[:, 0:HW].rearrange("p (h d) -> p h d", d=HD),
                                                      rden[:, :].unsqueeze(2).broadcast_to([P, HH, HD]), ALU.mult).then_inc(ov_free, 1)
                                    dve.wait_ge(ov_free, n.next("ov"))
                                    rows = xs[:, b, qt, hf * HW:(hf + 1) * HW]
                                    dve.tensor_tensor(rows, rows, ov[:, :], ALU.add).then_inc(x_upd, 1)
                                    n.next("upd")
                            yield
                        n.next("pv", NU)

                    round_of_two(norm, route, experts, finish, half)
            clear_all()


def kernel(**inputs):
    import concourse.bacc as _bacc
    from concourse.bass_utils import run_bass_kernel_spmd as _run

    a = {k: np.asarray(v) for k, v in inputs.items()}
    pre = "L0_attn_a_"
    mats_a = np.concatenate([a[pre + k] for k in ("w_y", "w_x", "w_ig", "w_ag", "w_out")], axis=1)
    q, k, v = (a["L0_attn_b_" + n].T for n in ("wq", "wk", "wv"))
    w_qkv = np.concatenate([m[:, hf * HW:(hf + 1) * HW] for hf in range(2) for m in (q, k, v)], axis=1)
    w1 = np.zeros((D, HID), np.float32)
    w1[:, 0:E * H] = a["L0_ffn_w1"].transpose(1, 0, 2).reshape(D, E * H)
    w1[:, E * H:(E + 1) * H] = a["L0_ffn_sw1"][0]
    w2 = np.zeros((HID, D), np.float32)
    w2[0:E * H] = a["L0_ffn_w2"].reshape(E * H, D)
    w2[E * H:(E + 1) * H] = a["L0_ffn_sw2"][0]
    rows = [a[pre + k] for k in ("b_y", "b_x", "conv_b", "a_param", "b_ig", "b_ag")] + list(a[pre + "conv_w"])
    vecs = np.stack(rows).reshape(NVEC, 2, P).transpose(2, 0, 1).reshape(P, NVEC * 2)
    sel = np.tile(np.repeat(np.eye(E, dtype=np.float32), H, axis=1), (2, 1))
    arrays = {
        "x": a[pre + "x"], "mats_a": mats_a, "w_qkv": w_qkv, "gate_w": a["L0_ffn_gate_w"].T, "w1": w1, "w2": w2,
        "vecs": vecs, "b_out": a[pre + "b_out"], "tau": a["L0_attn_b_tau"], "nu": a["L0_attn_b_nu"], "sel": sel,
    }
    arrays = {k: np.ascontiguousarray(v) for k, v in arrays.items()}
    nc = _bacc.Bacc("TRN2", target_bir_lowering=False, num_devices=1)
    args = [nc.dram_tensor(k, v.shape, mybir.dt.from_np(v.dtype), kind="ExternalInput").ap() for k, v in arrays.items()]
    out = nc.dram_tensor("out", (B, T, D), F32, kind="ExternalOutput").ap()
    hybrid_kernel(nc, *args, out)
    r = _run(nc, [arrays], core_ids=[0])
    return r.results[0]["out"]
```

```python
from contextlib import ExitStack

import concourse.bass as bass
import numpy as np
from concourse import mybir

ALU = mybir.AluOpType
ACT = mybir.ActivationFunctionType
F32 = mybir.dt.float32
F32R = mybir.dt.float32r
BF16 = mybir.dt.bfloat16
U32 = mybir.dt.uint32
I32 = mybir.dt.int32
AX_X = mybir.AxisListType.X

P = 128
B, T, D = 4, 512, 256
KD = D // P
TT = T // P
L = 256
TAPS = 4
E, H, TOPK = 16, 176, 2
G = 4
GS = E // G
NCH = -(-(E + 1) * H // P)
NROUTED = E * H // P
HID = NCH * P
assert E * H == NROUTED * P
HEADS, HD = 16, 16
HH = HEADS // 2
HP = HH // 2
HW = HH * HD
PAIR = 2
LN_EPS = 1e-5
L2_EPS = 1e-8
TOP_EPS = 1e-20
NEG = -1.0e30
NVEC = 10
(V_BY, V_BX, V_CB, V_AP, V_BIG, V_BAG, V_CW) = range(7)
MATS_A = 5
M_Y, M_X, M_IG, M_AG, M_OUT = range(MATS_A)


class Count:

    def __init__(self):
        self.n = {}

    def next(self, name, by=1):
        self.n[name] = self.n.get(name, 0) + by
        return self.n[name]

    def before(self, name):
        n = self.n.get(name, 0)
        self.n[name] = n + 1
        return n


def weave(main, n_main, side, n_side):
    done = 0
    for i in range(n_main):
        next(main)
        while done * n_main < (i + 1) * n_side:
            next(side)
            done += 1
    for rest in (main, side):
        assert next(rest, "end") == "end"


def run_all(steps):
    for _ in steps:
        pass


def hybrid_kernel(nc, x, mats_a, w_qkv, gate_w, w1, w2, vecs, b_out, tau, nu, sel, out):
    ctx = ExitStack()
    with ctx:
        def sb(name, shape, dt=F32, on=ctx):
            return on.enter_context(nc.sbuf_tensor(name, shape, dt))

        sems = []

        def sem(name):
            s = ctx.enter_context(nc.semaphore(name))
            sems.append(s)
            return s

        banks = [ctx.enter_context(nc.psum_tensor(f"bank{i}", [P, 512], F32)) for i in range(8)]

        w1h = sb("w1h", [P, KD, HID], F32R)
        w1l = sb("w1l", [P, KD, HID], F32R)
        w2h = sb("w2h", [P, NCH, D], F32R)
        w2l = sb("w2l", [P, NCH, D], F32R)
        wqkv = [sb(f"wqkv{i}", [P, KD, 3 * D], F32R) for i in range(2)]
        gw = [sb(f"gw{i}", [P, KD, E], F32R) for i in range(2)]
        selr = sb("selr", [P, NROUTED * P], F32R)
        xTh = [sb(f"xTh{b}", [P, KD, T], F32R) for b in range(PAIR)]
        xTl = [sb(f"xTl{b}", [P, KD, T], F32R) for b in range(PAIR)]
        ident = sb("ident", [P, P])
        identb = sb("identb", [P, P], BF16)
        maskb = sb("maskb", [P, P], BF16)
        mv = sb("mv", [P, TT, 2])
        stats = sb("stats", [P, TT, 6])
        vare = sb("vare", [P, TT])
        rstd = sb("rstd", [P, TT])
        mhalf = sb("mhalf", [P, TT])
        phalf = sb("phalf", [P, 3 * HH])
        taub = sb("taub", [P, 1])
        nub = sb("nub", [P, 1])

        x_rows = x.rearrange("b (t p) d -> b p t d", p=P)
        out_rows = out.rearrange("b (t p) d -> b p t d", p=P)

        def clear_all():
            for s in sems:
                nc.sync.sem_clear(s)
            nc.all_engine_barrier()

        QA = B
        W1Q, W2Q = HID // QA, NCH // QA
        a_ctx = ExitStack()
        with a_ctx:
            def sba(name, shape, dt=F32):
                return sb(name, shape, dt, a_ctx)

            wa = [sba(f"wa{i}", [P, KD, MATS_A * L], F32R) for i in range(2)]
            vec = sba("vec", [P, NVEC * 2])
            nsp = sba("nsp", [P, 2])
            sp1 = sba("sp1", [P, 2])
            sp2 = sba("sp2", [P, 2])
            one = sba("one", [P, 1])
            boutb = sba("boutb", [P, D])

            def v(which, m):
                return vec[:, 2 * which + m:2 * which + m + 1]

            p_ctx = ExitStack()
            with p_ctx:
                stage_a = sb("stage_a", [P, KD, MATS_A * L], F32, p_ctx)
                stage_q = sb("stage_q", [P, KD, 3 * D], F32, p_ctx)
                stage_g = sb("stage_g", [P, KD, E], F32, p_ctx)
                p_wa, p_q, p_g, p_v, p_b, p_id, p_act, p_vec, p_self, p_hi = (
                    sem(n) for n in ("p_wa", "p_q", "p_g", "p_v", "p_b", "p_id", "p_act", "p_vec", "p_self", "p_hi"))
                with nc.Block() as block:
                    @block.sync
                    def _(sp):
                        sp.dma_start(vec[:, :], vecs).then_inc(p_v, 16)
                        for kk in range(KD):
                            sp.dma_start(stage_a[:, kk, :], mats_a[kk * P:(kk + 1) * P, :]).then_inc(p_wa, 16)
                        for kk in range(KD):
                            sp.dma_start(stage_q[:, kk, :], w_qkv[kk * P:(kk + 1) * P, :]).then_inc(p_q, 16)
                        for kk in range(KD):
                            sp.dma_start(stage_g[:, kk, :], gate_w[kk * P:(kk + 1) * P, :]).then_inc(p_g, 16)
                        sp.dma_start(boutb[:, :], b_out.rearrange("(o d) -> o d", o=1).broadcast_to([P, D])).then_inc(p_b, 16)
                        sp.dma_start(taub[:, :], tau.rearrange("(o d) -> o d", o=1).broadcast_to([P, 1])).then_inc(p_b, 16)
                        sp.dma_start(nub[:, :], nu.rearrange("(o d) -> o d", o=1).broadcast_to([P, 1])).then_inc(p_b, 16)
                        sp.wait_ge(p_b, 48)

                    @block.gpsimd
                    def _(pool):
                        pool.memset(ident[:, :], 0.0).then_inc(p_id, 1)
                        pool.memset(maskb[:, :], 0.0).then_inc(p_id, 1)
                        pool.memset(mhalf[:, :], -0.5).then_inc(p_id, 1)
                        pool.memset(phalf[:, :], 0.5).then_inc(p_id, 1)
                        pool.memset(one[:, :], 1.0).then_inc(p_id, 1)
                        pool.wait_ge(p_id, 5)
                        pool.affine_select(out=ident[:, :], in_=ident[:, :], compare_op=ALU.not_equal, fill=1.0,
                                           base=0, pattern=[[-1, P]], channel_multiplier=1).then_inc(p_id, 1)
                        pool.affine_select(out=maskb[:, :], in_=maskb[:, :], compare_op=ALU.is_ge, fill=NEG,
                                           base=0, pattern=[[-1, P]], channel_multiplier=1).then_inc(p_id, 1)
                        pool.wait_ge(p_id, 7)
                        pool.tensor_copy(identb[:, :], ident[:, :]).then_inc(p_id, 1)
                        pool.wait_ge(p_hi, 2)
                        pool.tensor_tensor(wqkv[1][:, :, :], stage_q[:, :, :], wqkv[0][:, :, :].bitcast(F32),
                                           ALU.subtract).then_inc(p_id, 1)
                        pool.tensor_tensor(gw[1][:, :, :], stage_g[:, :, :], gw[0][:, :, :].bitcast(F32),
                                           ALU.subtract).then_inc(p_id, 1)

                    @block.scalar
                    def _(act):
                        act.wait_ge(p_v, 16)
                        act.activation(sp1[:, :], vec[:, 2 * V_AP:2 * V_AP + 2], ACT.Abs).then_inc(p_act, 1)
                        act.wait_ge(p_act, 1)
                        act.activation(sp2[:, :], sp1[:, :], ACT.Exp, scale=-1.0).then_inc(p_act, 1)
                        act.wait_ge(p_act, 2)
                        act.wait_ge(p_id, 5)
                        act.activation(sp1[:, :], sp2[:, :], ACT.Ln, bias=one[:, :]).then_inc(p_act, 1)
                        act.wait_ge(p_q, 16 * KD)
                        act.activation(wqkv[0][:, :, :], stage_q[:, :, :], ACT.Copy).then_inc(p_hi, 1)
                        act.wait_ge(p_g, 16 * KD)
                        act.activation(gw[0][:, :, :], stage_g[:, :, :], ACT.Copy).then_inc(p_hi, 1)

                    @block.vector
                    def _(dve):
                        for kk in range(KD):
                            dve.wait_ge(p_wa, 16 * KD)
                            dve.tensor_copy(wa[0][:, kk, :], stage_a[:, kk, :]).then_inc(p_self, 1)
                            dve.wait_ge(p_self, 2 * kk + 1)
                            dve.tensor_tensor(wa[1][:, kk, :], stage_a[:, kk, :], wa[0][:, kk, :].bitcast(F32),
                                              ALU.subtract).then_inc(p_self, 1)
                        dve.wait_ge(p_act, 3)
                        dve.scalar_tensor_tensor(out=nsp[:, :], in0=vec[:, 2 * V_AP:2 * V_AP + 2], scalar=0.0,
                                                 in1=sp1[:, :], op0=ALU.max, op1=ALU.add).then_inc(p_self, 1)
                        dve.wait_ge(p_self, 2 * KD + 1)
                        dve.tensor_scalar(nsp[:, :], nsp[:, :], -8.0, None, ALU.mult).then_inc(p_self, 1)
                clear_all()

            xs = sba("xs_a", [P, TT, D])
            xn = sba("xn_a", [P, TT, D])
            st1 = sba("st1", [P, KD, W1Q])
            st2 = sba("st2", [P, W2Q, D])
            xb = sba("xb", [P, 2, TAPS - 1 + T])
            cv = sba("cv", [P, 2, T])
            sh = sba("sh", [P, 2, T], F32R)
            sl = sba("sl", [P, 2, T], F32R)
            gx = sba("gx", [P, 2, T])
            av = sba("av", [P, 2, T])
            yv = sba("yv", [P, 2, T])

            (a_x, a_w1, a_w2, a_out, a_ln, a_rstd, a_xn, a_tp, a_hi, a_lo, a_ps, a_xb, a_y, a_conv, a_chi, a_clo,
             a_gate, a_g, a_e, a_na, a_m, a_hy, a_hyh, a_hyl, a_o, a_xr, a_wh, a_wl, a_self, a_pool, a_xsum,
             a_tfree) = (
                sem(n) for n in (
                    "a_x", "a_w1", "a_w2", "a_out", "a_ln", "a_rstd", "a_xn", "a_tp", "a_hi", "a_lo", "a_ps", "a_xb",
                    "a_y", "a_conv", "a_chi", "a_clo", "a_gate", "a_g", "a_e", "a_na", "a_m", "a_hy", "a_hyh",
                    "a_hyl", "a_o", "a_xr", "a_wh", "a_wl", "a_self", "a_pool", "a_xsum", "a_tfree"))

            bT, bXB, bG, bY = (0, 1), (2, 3), (4, 5, 6, 7), (0, 1)
            with nc.Fori(0, B) as it:
                with nc.Block() as block:
                    @block.sync
                    def _(sp):
                        sp.dma_start(xs[:, :, :], x_rows[bass.ds(it, 1), :, :, :].rearrange("o p t d -> (o p) t d")).then_inc(a_x, 16)
                        for kk in range(KD):
                            sp.dma_start(st1[:, kk, :], w1[kk * P:(kk + 1) * P, bass.ds(it * W1Q, W1Q)]).then_inc(a_w1, 16)
                        sp.dma_start(st2[:, :, :], w2.rearrange("(q c p) d -> q p c d", p=P, q=QA)[bass.ds(it, 1), :, :, :]
                                     .rearrange("o p c d -> (o p) c d")).then_inc(a_w2, 16)
                        sp.wait_ge(a_xsum, TT)
                        sp.dma_start(out_rows[bass.ds(it, 1), :, :, :].rearrange("o p t d -> (o p) t d"), xs[:, :, :]).then_inc(a_out, 16)
                        sp.wait_ge(a_out, 16)

                    @block.gpsimd
                    def _(pool):
                        pool.wait_ge(a_ln, TT)
                        pool.tensor_scalar(vare[:, :], mv[:, :, 1], LN_EPS, None, ALU.add).then_inc(a_pool, 1)
                        pool.wait_ge(a_pool, 1)
                        pool.tensor_tensor(rstd[:, :], vare[:, :], mhalf[:, :], ALU.pow).then_inc(a_rstd, 1)
                        pool.wait_ge(a_xn, TT)
                        for t in range(TT):
                            pool.tensor_tensor(xs[:, t, :], xs[:, t, :], boutb[:, :], ALU.add).then_inc(a_xr, 1)
                        pool.wait_ge(a_wh, 1)
                        pool.tensor_tensor(w1l[:, :, bass.ds(it * W1Q, W1Q)], st1[:, :, :],
                                           w1h[:, :, bass.ds(it * W1Q, W1Q)].bitcast(F32), ALU.subtract).then_inc(a_wl, 1)
                        pool.wait_ge(a_wh, 2)
                        pool.tensor_tensor(w2l[:, bass.ds(it * W2Q, W2Q), :], st2[:, :, :],
                                           w2h[:, bass.ds(it * W2Q, W2Q), :].bitcast(F32), ALU.subtract).then_inc(a_wl, 1)

                    @block.scalar
                    def _(act):
                        for kk in range(KD):
                            act.wait_ge(a_tp, kk + 1)
                            act.activation(xTh[0][:, kk, :], banks[bT[kk]][:, :], ACT.Copy).then_inc(a_hi, 1)
                        for m in range(2):
                            act.wait_ge(a_ps, m + 1)
                            act.activation(xb[:, m, TAPS - 1:], banks[bXB[m]][:, :], ACT.Identity, bias=v(V_BX, m)).then_inc(a_xb, 1)
                        for m in range(2):
                            act.wait_ge(a_ps, m + 3)
                            act.activation(yv[:, m, :], banks[bY[m]][:, :], ACT.Gelu, bias=v(V_BY, m)).then_inc(a_y, 1)
                        for m in range(2):
                            act.wait_ge(a_conv, m + 1)
                            act.activation(sh[:, m, :], cv[:, m, :], ACT.Copy).then_inc(a_chi, 1)
                        act.wait_ge(a_w1, 16 * KD)
                        act.activation(w1h[:, :, bass.ds(it * W1Q, W1Q)], st1[:, :, :], ACT.Copy).then_inc(a_wh, 1)
                        for j in range(4):
                            dst, b = ((gx, V_BIG), (av, V_BAG))[j // 2]
                            act.wait_ge(a_gate, j + 1)
                            act.activation(dst[:, j % 2, :], banks[bG[j]][:, :], ACT.Sigmoid, bias=v(b, j % 2)).then_inc(a_g, 1)
                        act.wait_ge(a_g, 4)
                        for m in range(2):
                            act.activation(av[:, m, :], av[:, m, :], ACT.Exp, scale=nsp[:, m:m + 1]).then_inc(a_e, 1)
                        for m in range(2):
                            act.wait_ge(a_na, m + 1)
                            act.activation(xb[:, m, TAPS - 1:], xb[:, m, TAPS - 1:], ACT.Sqrt, bias=one[:, :]).then_inc(a_m, 1)
                        act.wait_ge(a_w2, 16)
                        act.activation(w2h[:, bass.ds(it * W2Q, W2Q), :], st2[:, :, :], ACT.Copy).then_inc(a_wh, 1)
                        for m in range(2):
                            act.wait_ge(a_hy, m + 1)
                            act.activation(sh[:, m, :], yv[:, m, :], ACT.Copy).then_inc(a_hyh, 1)

                    @block.vector
                    def _(dve):
                        n = Count()

                        def link(ins):
                            ins.then_inc(a_self, 1)
                            dve.wait_ge(a_self, n.next("self"))

                        dve.memset(xb[:, :, 0:TAPS - 1], 0.0).then_inc(a_self, 1)
                        n.next("self")
                        dve.wait_ge(a_x, 16)
                        for t in range(TT):
                            link(dve.bn_stats(stats[:, t, :], xs[:, t, :]))
                            dve.bn_aggr(mv[:, t, :], stats[:, t, :]).then_inc(a_ln, 1)
                        dve.wait_ge(a_rstd, 1)
                        for t in range(TT):
                            dve.tensor_scalar(xn[:, t, :], xs[:, t, :], mv[:, t, 0:1], rstd[:, t:t + 1],
                                              ALU.subtract, ALU.mult).then_inc(a_xn, 1)
                        for kk in range(KD):
                            dve.wait_ge(a_hi, kk + 1)
                            dve.tensor_tensor(xTl[0][:, kk, :], banks[bT[kk]][:, :], xTh[0][:, kk, :].bitcast(F32),
                                              ALU.subtract).then_inc(a_lo, 1)
                        for m in range(2):
                            dve.wait_ge(a_xb, m + 1)
                            link(dve.tensor_scalar(cv[:, m, :], xb[:, m, TAPS - 1:], v(V_CW + TAPS - 1, m), v(V_CB, m),
                                                   ALU.mult, ALU.add))
                            for k in range(TAPS - 1):
                                last = dve.scalar_tensor_tensor(out=cv[:, m, :], in0=xb[:, m, k:k + T], scalar=v(V_CW + k, m),
                                                                in1=cv[:, m, :], op0=ALU.mult, op1=ALU.add)
                                if k < TAPS - 2:
                                    link(last)
                            last.then_inc(a_conv, 1)
                            dve.wait_ge(a_chi, m + 1)
                            dve.tensor_tensor(sl[:, m, :], cv[:, m, :], sh[:, m, :].bitcast(F32), ALU.subtract).then_inc(a_clo, 1)
                        for m in range(2):
                            dve.wait_ge(a_g, m + 1)
                            link(dve.tensor_tensor(gx[:, m, :], gx[:, m, :], cv[:, m, :], ALU.mult))
                        for m in range(2):
                            dve.wait_ge(a_e, m + 1)
                            link(dve.memset(av[:, m, 0:1], 0.0))
                            dve.scalar_tensor_tensor(out=xb[:, m, TAPS - 1:], in0=av[:, m, :], scalar=-1.0,
                                                     in1=av[:, m, :], op0=ALU.mult, op1=ALU.mult).then_inc(a_na, 1)
                        for m in range(2):
                            dve.wait_ge(a_m, m + 1)
                            link(dve.tensor_tensor(gx[:, m, :], gx[:, m, :], xb[:, m, TAPS - 1:], ALU.mult))
                            link(dve.tensor_tensor_scan(cv[:, m, :], av[:, m, :], gx[:, m, :], 0.0, ALU.mult, ALU.add))
                            dve.wait_ge(a_y, m + 1)
                            dve.tensor_tensor(yv[:, m, :], cv[:, m, :], yv[:, m, :], ALU.mult).then_inc(a_hy, 1)
                            dve.wait_ge(a_hyh, m + 1)
                            dve.tensor_tensor(sl[:, m, :], yv[:, m, :], sh[:, m, :].bitcast(F32), ALU.subtract).then_inc(a_hyl, 1)
                        for t in range(TT):
                            dve.wait_ge(a_xr, t + 1)
                            dve.wait_ge(a_o, t + 1)
                            dve.tensor_tensor(xs[:, t, :], banks[bG[t]][:, 0:D], xs[:, t, :], ALU.add).then_inc(a_xsum, 1)

                    @block.tensor
                    def _(pe):
                        pe.wait_ge(a_xn, TT)
                        for kk in range(KD):
                            for t in range(TT):
                                last = pe.transpose(banks[bT[kk]][:, t * P:(t + 1) * P], xn[:, t, kk * P:(kk + 1) * P], ident[:, :])
                            last.then_inc(a_tp, 1)

                        def product(bank, mat, m, hi, lo):
                            for kk in range(KD):
                                w = [wa[i][:, kk, mat * L + m * P:mat * L + (m + 1) * P] for i in range(2)]
                                pe.matmul(bank, w[0], hi[:, kk, :], start=(kk == 0), stop=False)
                                pe.matmul(bank, w[1], hi[:, kk, :], start=False, stop=False)
                                last = pe.matmul(bank, w[0], lo[:, kk, :], start=False, stop=(kk == KD - 1))
                            return last

                        pe.wait_ge(a_hi, KD)
                        pe.wait_ge(a_lo, KD)
                        for m in range(2):
                            product(banks[bXB[m]][:, :], M_X, m, xTh[0], xTl[0]).then_inc(a_ps, 1)
                        for m in range(2):
                            product(banks[bY[m]][:, :], M_Y, m, xTh[0], xTl[0]).then_inc(a_ps, 1)
                        pe.wait_ge(a_chi, 2)
                        pe.wait_ge(a_clo, 2)
                        for j in range(4):
                            product(banks[bG[j]][:, :], (M_IG, M_AG)[j // 2], j % 2, sh, sl).then_inc(a_gate, 1)
                        pe.wait_ge(a_hyh, 2)
                        pe.wait_ge(a_hyl, 2)
                        for t in range(TT):
                            for kk in range(KD):
                                w = [wa[i][:, kk, M_OUT * L:(M_OUT + 1) * L] for i in range(2)]
                                tok = slice(t * P, (t + 1) * P)
                                pe.matmul(banks[bG[t]][:, 0:D], sh[:, kk, tok], w[0], start=(kk == 0), stop=False)
                                pe.matmul(banks[bG[t]][:, 0:D], sh[:, kk, tok], w[1], start=False, stop=False)
                                last = pe.matmul(banks[bG[t]][:, 0:D], sl[:, kk, tok], w[0], start=False, stop=(kk == KD - 1))
                            last.then_inc(a_o, 1)
                clear_all()

        Z, CWB, ACC, SC, TP, OV = banks[0], banks[1], banks[2:4], banks[4:6], banks[6], banks[7]

        xs = sb("xs", [P, PAIR, TT, D])
        big = sb("big", [P, TT * D])
        xn = big[:, :].rearrange("p (t d) -> p t d", t=TT)
        yT = big[:, :].rearrange("p (m t) -> p m t", m=KD)
        spare = big[:, TT * D // 2:]
        pmx, pmn = (spare[:, i * TT * G * 2:(i + 1) * TT * G * 2].rearrange("p (t g e) -> p t g e", t=TT, g=G) for i in range(2))
        gcmp, gcm2 = (spare[:, (i + 1) * TT * G * G:(i + 2) * TT * G * G].rearrange("p (t g e) -> p t g e", t=TT, g=G) for i in range(2))
        cw, cw2 = (spare[:, (i + 3) * TT * E:(i + 4) * TT * E].rearrange("p (t e) -> p t e", t=TT) for i in range(2))
        ov = big[:, 0:HW]
        th = sb("th", [P, 2, T])
        tv = sb("tv", [P, 2, T])
        tvh = sb("tvh", [P, 2, T], F32R)
        tvl = sb("tvl", [P, 2, T], F32R)
        cT = [sb(f"cT{b}", [P, T], F32R) for b in range(PAIR)]
        score = sb("score", [P, TT, G, GS])
        gsum = sb("gsum", [P, TT, G])
        gbest = sb("gbest", [P, TT, G])
        tri = sb("tri", [P, G, G])
        iot = sb("iot", [P, E])
        top8 = sb("top8", [P, TT, 8])
        idx8 = sb("idx8", [P, TT, 8], U32)
        idxf = sb("idxf", [P, TT, TOPK])
        wsum = sb("wsum", [P, TT])
        wtop = sb("wtop", [P, TT, TOPK])
        cc = sb("cc", [P, TT, P], F32R)
        raw = sb("raw", [P, TT, 3 * HW])
        nrm = sb("nrm", [P, TT, 3 * HH])
        nrt = sb("nrt", [P, TT, 3 * HH])
        nry = sb("nry", [P, TT, 3 * HH])
        vt = raw[:, :, 2 * HW:]
        stq = sb("stq", [P, HH, 4, HD], F32R)
        stk = sb("stk", [P, HH, 4, HD], F32R)
        qT = sb("qT", [P, HP, T], F32R)
        kT = sb("kT", [P, HP, T], F32R)
        pr = sb("pr", [P, 2, T])
        sq = pr[:, :, 0:3 * HW]
        prT = sb("prT", [P, 2, T])
        nmax = sb("nmax", [P, 2])
        den = sb("den", [P, 2, HH])
        rden = sb("rden", [P, HH])

        UNITS = [(qt, h) for qt in range(TT) for h in range(HH)]
        NU = len(UNITS)
        N_EXPERTS = 3 * (NCH + 2)
        N_LN, N_ROUTE, N_FIN = 6, 8, 4
        N_PREP = 2 * TT + 6
        N_HALF = N_PREP + NU + 4
        X_EXPERTS, X_ATTENTION = 2, 2 * TT

        def evacuates(u):
            return "dve" if u % 3 == 2 else "act"

        (x_in, x_out, c_sel, c_pool, self_dve, self_pool, ln_stats, rstd_ok, xn_ok, xt_ps, xt_hi, xt_lo, rt_ps,
         rt_exp, comb_ok, ct_ps, ct_ok, z_full, tanh_ok, z_used, c_full, t_ok, th_ok, tl_ok, o_done, acc_out,
         fin_ps, x_upd, qkv_ps, sq_ok, raw_ok, sq_used, st_ok, stT_ps, qkT_ok, sc_ps,
         max_ok, p_ok, pT_ps, pT_ok, pv_ps, ov_free) = (
            sem(name) for name in (
                "x_in", "x_out", "c_sel", "c_pool", "self_dve", "self_pool", "ln_stats", "rstd_ok", "xn_ok",
                "xt_ps", "xt_hi", "xt_lo", "rt_ps", "rt_exp", "comb_ok", "ct_ps", "ct_ok", "z_full", "tanh_ok",
                "z_used", "c_full", "t_ok", "th_ok", "tl_ok", "o_done", "acc_out", "fin_ps", "x_upd", "qkv_ps",
                "sq_ok", "raw_ok", "sq_used", "st_ok", "stT_ps", "qkT_ok", "sc_ps",
                "max_ok", "p_ok", "pT_ps", "pT_ok", "pv_ps", "ov_free"))

        SELC = NROUTED * P // 4
        assert SELC <= TT * D
        with nc.Block() as block:
            @block.gpsimd
            def _(pool):
                pool.memset(tri[:, :, :], 1.0).then_inc(c_pool, 1)
                pool.memset(cc[:, :, :].bitcast(F32), 0.0).then_inc(c_pool, 1)
                pool.iota(iot[:, :], pattern=[[1, E]], base=0, channel_multiplier=0,
                          allow_small_or_imprecise_dtypes=True).then_inc(c_pool, 1)
                pool.wait_ge(c_pool, 3)
                pool.affine_select(out=tri[:, :, :], in_=tri[:, :, :], compare_op=ALU.is_gt, fill=0.0,
                                   base=0, pattern=[[1, G], [-1, G]], channel_multiplier=0).then_inc(c_pool, 1)

            @block.sync
            def _(sp):
                for j in range(4):
                    sp.wait_ge(c_sel, j + 1)
                    sp.dma_start(big[0:2 * E, 0:SELC], sel[:, j * SELC:(j + 1) * SELC]).then_inc(x_in, 16)

            @block.vector
            def _(dve):
                dve.memset(big[:, :], 0.0).then_inc(c_sel, 1)
                for j in range(4):
                    dve.wait_ge(x_in, 16 * (j + 1))
                    dve.tensor_copy(selr[:, j * SELC:(j + 1) * SELC], big[:, 0:SELC]).then_inc(c_sel, 1)
        clear_all()

        def round_of_two(norm, route, experts, finish, half):
            def attention(b):
                yield from finish(b)
                yield from norm(b)
                yield from half(b, 0)
                yield from half(b, 1)
                yield from norm(b)
                yield from route(b)

            def norm_route(b):
                yield from norm(b)
                yield from route(b)

            n_attention = N_FIN + 2 * N_LN + 2 * N_HALF + N_ROUTE
            for _ in norm_route(0):
                pass
            weave(experts(0), N_EXPERTS, norm_route(1), N_LN + N_ROUTE)
            weave(experts(1), N_EXPERTS, attention(0), n_attention)
            weave(experts(0), N_EXPERTS, attention(1), n_attention)
            weave(experts(1), N_EXPERTS, finish(0), N_FIN)
            for _ in finish(1):
                pass

        with nc.Fori(0, B // PAIR) as it:
            with nc.Block() as block:
                @block.sync
                def _(sp):
                    for b in range(PAIR):
                        sp.dma_start(xs[:, b, :, :], out_rows[bass.ds(it * PAIR + b, 1), :, :, :]
                                     .rearrange("o p t d -> (o p) t d")).then_inc(x_in, 16)
                    for b in range(PAIR):
                        sp.wait_ge(x_upd, PAIR * (X_EXPERTS + X_ATTENTION) + (b + 1) * X_EXPERTS)
                        sp.dma_start(out_rows[bass.ds(it * PAIR + b, 1), :, :, :].rearrange("o p t d -> (o p) t d"),
                                     xs[:, b, :, :]).then_inc(x_out, 16)
                    sp.wait_ge(x_out, 16 * PAIR)

                @block.tensor
                def _(pe):
                    n = Count()

                    def split_product(o, a, b, start, stop):
                        pe.matmul(o, a[0], b[0], start=start, stop=False)
                        pe.matmul(o, a[1], b[0], start=False, stop=False)
                        return pe.matmul(o, a[0], b[1], start=False, stop=stop)

                    def norm(b):
                        for _ in range(3):
                            yield
                        pe.wait_ge(xn_ok, n.next("xn", TT))
                        for kk in range(KD):
                            for t in range(TT):
                                last = pe.transpose(SC[kk][:, t * P:(t + 1) * P], xn[:, t, kk * P:(kk + 1) * P], ident[:, :])
                            last.then_inc(xt_ps, 1)
                            yield
                        pe.wait_ge(xt_lo, n.next("xt_lo", KD))
                        yield

                    def route(b):
                        for t in range(TT):
                            tok = slice(t * P, (t + 1) * P)
                            for kk in range(KD):
                                last = split_product(TP[:, t * E:(t + 1) * E], (xTh[b][:, kk, tok], xTl[b][:, kk, tok]),
                                                     (gw[0][:, kk, :], gw[1][:, kk, :]), kk == 0, kk == KD - 1)
                        last.then_inc(rt_ps, 1)
                        for _ in range(N_ROUTE - 2):
                            yield
                        pe.wait_ge(comb_ok, n.next("comb"))
                        for t in range(TT):
                            last = pe.transpose(TP[:, t * P:(t + 1) * P], cc[:, t, :].bitcast(F32), ident[:, :])
                        last.then_inc(ct_ps, 1)
                        yield
                        yield

                    def experts(b):
                        pe.wait_ge(ct_ok, n.next("ct"))
                        inst = n.before("experts")
                        for c in range(NCH + 2):
                            g = inst * NCH + c
                            if c < NCH:
                                hid = slice(c * P, (c + 1) * P)
                                if g:
                                    pe.wait_ge(z_used, g)
                                for kk in range(KD):
                                    last = split_product(Z[:, :], (w1h[:, kk, hid], w1l[:, kk, hid]),
                                                         (xTh[b][:, kk, :], xTl[b][:, kk, :]), kk == 0, kk == KD - 1)
                                last.then_inc(z_full, 1)
                            if c < NROUTED:
                                if g:
                                    pe.wait_ge(t_ok, g)
                                pe.matmul(CWB[:, :], selr[:, c * P:(c + 1) * P], cT[b][:, :], start=True, stop=True).then_inc(c_full, 1)
                            yield
                            if c >= 2:
                                if c == 2 and inst:
                                    pe.wait_ge(acc_out, KD * inst)
                                pe.wait_ge(tl_ok, g - 1)
                            for m in range(KD):
                                if c >= 2:
                                    k = g % 2
                                    last = split_product(ACC[m][:, :], (w2h[:, c - 2, m * P:(m + 1) * P], w2l[:, c - 2, m * P:(m + 1) * P]),
                                                         (tvh[:, k, :], tvl[:, k, :]), c == 2, c == NCH + 1)
                                    if m == KD - 1:
                                        last.then_inc(o_done, 1)
                                yield

                    def finish(b):
                        yield
                        pe.wait_ge(acc_out, n.next("acc", KD))
                        for j in range(2):
                            for t in range(2):
                                for kk in range(KD):
                                    last = pe.transpose(SC[j][:, t * D + kk * P:t * D + (kk + 1) * P],
                                                        yT[:, kk, (2 * j + t) * P:(2 * j + t + 1) * P], ident[:, :])
                            last.then_inc(fin_ps, 1)
                            yield
                        yield

                    def half(b, hf):
                        cols = slice(hf * 3 * HW, (hf + 1) * 3 * HW)
                        for i in range(N_PREP):
                            if i < TT:
                                t = i
                                if t >= 2:
                                    pe.wait_ge(raw_ok, n.n.get("raw", 0) + t - 1)
                                tok = slice(t * P, (t + 1) * P)
                                for kk in range(KD):
                                    last = split_product(SC[t % 2][:, 0:3 * HW], (xTh[b][:, kk, tok], xTl[b][:, kk, tok]),
                                                         (wqkv[0][:, kk, cols], wqkv[1][:, kk, cols]), kk == 0, kk == KD - 1)
                                last.then_inc(qkv_ps, 1)
                            if i == TT:
                                n.next("raw", TT)
                            if i >= TT + 6:
                                t = i - TT - 6
                                pe.wait_ge(st_ok, n.next("st", 2))
                                k = n.n.get("qkT", 0) + 2 * t
                                if k:
                                    pe.wait_ge(qkT_ok, k)
                                for bank, st in ((TP, stq), (OV, stk)):
                                    rows = st[:, :, :, :].bitcast(F32).rearrange("p (j h) f d -> p j (h f d)", h=2)
                                    if bank is OV and t == 0 and n.n.get("ov", 0):
                                        pe.wait_ge(ov_free, n.n["ov"])
                                    for j in range(HP):
                                        last = pe.transpose(bank[:, j * P:(j + 1) * P], rows[:, j, :], ident[:, :])
                                    last.then_inc(stT_ps, 1)
                            yield
                        pe.wait_ge(qkT_ok, n.next("qkT", 2 * TT))
                        for u in range(NU + 4):
                            if 3 <= u < NU + 3:
                                pe.wait_ge(pT_ok, n.next("pT"))
                            if 2 <= u < NU + 2:
                                qt, h = UNITS[u - 2]
                                pe.wait_ge(p_ok, n.next("p"))
                                for j in range(qt + 1):
                                    last = pe.transpose(TP[:, j * P:(j + 1) * P], pr[:, u % 2, j * P:(j + 1) * P], ident[:, :])
                                last.then_inc(pT_ps, 1)
                            if u < NU:
                                qt, h = UNITS[u]
                                w = (qt + 1) * P
                                r = slice((h % 2) * 64, (h % 2) * 64 + 64)
                                pe.matmul(SC[u % 2][:, 0:w], qT[r, h // 2, qt * P:(qt + 1) * P], kT[r, h // 2, 0:w],
                                          start=True, stop=False)
                                pe.matmul(SC[u % 2][:, w - P:w], identb[:, :], maskb[:, :], start=False, stop=True).then_inc(sc_ps, 1)
                            if 3 <= u < NU + 3:
                                qt, h = UNITS[u - 3]
                                if h == 0 and n.before("ov"):
                                    pe.wait_ge(ov_free, n.n["ov"] - 1)
                                for j in range(qt + 1):
                                    last = pe.matmul(OV[:, h * HD:(h + 1) * HD], prT[:, (u - 3) % 2, j * P:(j + 1) * P],
                                                     vt[:, j, h * HD:(h + 1) * HD], start=(j == 0), stop=(j == qt))
                                last.then_inc(pv_ps, 1)
                            yield

                    round_of_two(norm, route, experts, finish, half)

                @block.scalar
                def _(act):
                    n = Count()

                    def norm(b):
                        for _ in range(3):
                            yield
                        for kk in range(KD):
                            act.wait_ge(xt_ps, n.next("xt"))
                            act.activation(xTh[b][:, kk, :], SC[kk][:, :], ACT.Copy).then_inc(xt_hi, 1)
                            yield
                        yield

                    def route(b):
                        act.wait_ge(rt_ps, n.next("rt"))
                        act.activation(score[:, :, :, :].rearrange("p t g e -> p (t g e)"), TP[:, 0:TT * E], ACT.Exp,
                                       scale=-1.0).then_inc(rt_exp, 1)
                        for _ in range(N_ROUTE - 2):
                            yield
                        act.wait_ge(ct_ps, n.next("ct"))
                        act.activation(cT[b][:, :], TP[:, :], ACT.Copy).then_inc(ct_ok, 1)
                        yield
                        yield

                    def experts(b):
                        inst = n.before("experts")
                        for c in range(NCH + 2):
                            g = inst * NCH + c
                            if 1 <= c <= NCH:
                                act.wait_ge(t_ok, g)
                                if g >= 3:
                                    act.wait_ge(o_done, g - 2)
                                act.activation(tvh[:, (g - 1) % 2, :], tv[:, (g - 1) % 2, :], ACT.Copy).then_inc(th_ok, 1)
                            yield
                            if c < NCH:
                                act.wait_ge(z_full, g + 1)
                                act.activation(th[:, g % 2, :], Z[:, :], ACT.Tanh, scale=0.5).then_inc(tanh_ok, 1)
                            yield
                            yield

                    def finish(b):
                        act.wait_ge(o_done, n.next("fin", NCH))
                        act.activation(yT[:, 0, :], ACC[0][:, :], ACT.Copy).then_inc(acc_out, 1)
                        for _ in range(N_FIN):
                            yield

                    def half(b, hf):
                        for i in range(N_PREP):
                            if 1 <= i <= TT:
                                t = i - 1
                                act.wait_ge(qkv_ps, n.next("qkv"))
                                g = n.before("sq")
                                if g >= 2:
                                    act.wait_ge(sq_used, g - 1)
                                act.activation(sq[:, t % 2, :], SC[t % 2][:, 0:3 * HW], ACT.Square).then_inc(sq_ok, 1)
                                act.activation(raw[:, t, :], SC[t % 2][:, 0:3 * HW], ACT.Copy).then_inc(raw_ok, 1)
                            if i >= TT + 6:
                                t = i - TT - 6
                                for bank, dst in ((TP, qT), (OV, kT)):
                                    act.wait_ge(stT_ps, n.next("stT"))
                                    act.activation(dst[:, :, t * P:(t + 1) * P],
                                                   bank[:, :].rearrange("p (j q) -> p j q", j=HP), ACT.Copy).then_inc(qkT_ok, 1)
                            yield
                        for u in range(NU + 4):
                            if 2 <= u < NU + 2:
                                qt, h = UNITS[u - 2]
                                k = n.next("pT")
                                if evacuates(u - 2) == "act":
                                    act.wait_ge(pT_ps, k)
                                    act.activation(prT[:, u % 2, 0:(qt + 1) * P], TP[:, 0:(qt + 1) * P], ACT.Copy).then_inc(pT_ok, 1)
                            if 1 <= u <= NU:
                                qt, h = UNITS[u - 1]
                                w, k = (qt + 1) * P, (u - 1) % 2
                                act.wait_ge(max_ok, n.next("max"))
                                act.activation(pr[:, k, 0:w], SC[k][:, 0:w], ACT.Exp, bias=nmax[:, k:k + 1],
                                               accum_out=den[:, qt % 2, h:h + 1]).then_inc(p_ok, 1)
                            yield

                    round_of_two(norm, route, experts, finish, half)

                @block.gpsimd
                def _(pool):
                    n = Count()

                    def norm(b):
                        pool.wait_ge(ln_stats, n.next("ln", TT))
                        pool.tensor_scalar(vare[:, :], mv[:, :, 1], LN_EPS, None, ALU.add).then_inc(self_pool, 1)
                        pool.wait_ge(self_pool, n.next("self"))
                        pool.tensor_tensor(rstd[:, :], vare[:, :], mhalf[:, :], ALU.pow).then_inc(rstd_ok, 1)
                        for _ in range(N_LN):
                            yield

                    def route(b):
                        for _ in range(N_ROUTE):
                            yield

                    def experts(b):
                        for _ in range(N_EXPERTS):
                            yield

                    def finish(b):
                        for _ in range(N_FIN):
                            yield

                    def half(b, hf):
                        for _ in range(N_HALF):
                            yield

                    round_of_two(norm, route, experts, finish, half)

                @block.vector
                def _(dve):
                    n = Count()

                    def link(ins):
                        ins.then_inc(self_dve, 1)
                        dve.wait_ge(self_dve, n.next("self"))

                    def norm(b):
                        if n.n.get("upd", 0):
                            dve.wait_ge(x_upd, n.n["upd"])
                        else:
                            dve.wait_ge(x_in, 16 * PAIR)
                        for t in range(TT):
                            link(dve.bn_stats(stats[:, t, :], xs[:, b, t, :]))
                            dve.bn_aggr(mv[:, t, :], stats[:, t, :]).then_inc(ln_stats, 1)
                        yield
                        dve.wait_ge(rstd_ok, n.next("rstd"))
                        for t in range(TT):
                            dve.tensor_scalar(xn[:, t, :], xs[:, b, t, :], mv[:, t, 0:1], rstd[:, t:t + 1],
                                              ALU.subtract, ALU.mult).then_inc(xn_ok, 1)
                        yield
                        yield
                        for kk in range(KD):
                            dve.wait_ge(xt_hi, n.next("xt"))
                            dve.tensor_tensor(xTl[b][:, kk, :], SC[kk][:, :], xTh[b][:, kk, :].bitcast(F32),
                                              ALU.subtract).then_inc(xt_lo, 1)
                            yield
                        yield

                    def route(b):
                        flat = score[:, :, :, :].rearrange("p t g e -> p (t g e)")
                        dve.wait_ge(rt_exp, n.next("rt"))
                        link(dve.tensor_scalar(flat, flat, 1.0, None, ALU.add))
                        link(dve.reciprocal(flat, flat))
                        dve.tensor_tensor(pmx[:, :, :, :], score[:, :, :, 0:2], score[:, :, :, 2:4], ALU.max)
                        link(dve.tensor_tensor(pmn[:, :, :, :], score[:, :, :, 0:2], score[:, :, :, 2:4], ALU.min))
                        dve.tensor_tensor(gsum[:, :, :], pmx[:, :, :, 0], pmx[:, :, :, 1], ALU.max)
                        dve.tensor_tensor(gbest[:, :, :], pmx[:, :, :, 0], pmx[:, :, :, 1], ALU.min)
                        link(dve.tensor_tensor(pmn[:, :, :, 0], pmn[:, :, :, 0], pmn[:, :, :, 1], ALU.max))
                        link(dve.tensor_tensor(gbest[:, :, :], gbest[:, :, :], pmn[:, :, :, 0], ALU.max))
                        link(dve.tensor_tensor(gsum[:, :, :], gsum[:, :, :], gbest[:, :, :], ALU.add))
                        yield
                        shape = [P, TT, G, G]
                        other = gsum[:, :, :].unsqueeze(2).broadcast_to(shape)
                        own = gsum[:, :, :].unsqueeze(3).broadcast_to(shape)
                        dve.tensor_tensor(gcmp[:, :, :, :], other, own, ALU.is_gt)
                        link(dve.tensor_tensor(gcm2[:, :, :, :], other, own, ALU.is_ge))
                        link(dve.tensor_tensor(gcm2[:, :, :, :], gcm2[:, :, :, :],
                                               tri[:, :, :].unsqueeze(1).broadcast_to(shape), ALU.mult))
                        link(dve.tensor_tensor(gcmp[:, :, :, :], gcmp[:, :, :, :], gcm2[:, :, :, :], ALU.max))
                        link(dve.tensor_reduce(gbest[:, :, :], gcmp[:, :, :, :], AX_X, ALU.add))
                        link(dve.tensor_scalar(gbest[:, :, :], gbest[:, :, :], 2.0, None, ALU.is_lt))
                        link(dve.tensor_tensor(score[:, :, :, :], score[:, :, :, :],
                                               gbest[:, :, :].unsqueeze(3).broadcast_to([P, TT, G, GS]), ALU.mult))
                        yield
                        rows = score[:, :, :, :].rearrange("p t g e -> p t (g e)")
                        for t in range(TT):
                            link(dve.max(top8[:, t, :], rows[:, t, :]))
                        for t in range(TT):
                            last = dve.max_index(idx8[:, t, :], top8[:, t, :], rows[:, t, :])
                            if t == TT - 1:
                                link(last)
                        yield
                        dve.tensor_copy(idxf[:, :, :], idx8[:, :, 0:TOPK])
                        link(dve.tensor_tensor(wsum[:, :], top8[:, :, 0], top8[:, :, 1], ALU.add))
                        link(dve.tensor_scalar(wsum[:, :], wsum[:, :], TOP_EPS, None, ALU.add))
                        link(dve.reciprocal(wsum[:, :], wsum[:, :]))
                        link(dve.scalar_tensor_tensor(out=wtop[:, :, :], in0=top8[:, :, 0:TOPK], scalar=0.5,
                                                      in1=wsum[:, :].unsqueeze(2).broadcast_to([P, TT, TOPK]),
                                                      op0=ALU.mult, op1=ALU.mult))
                        yield
                        wide = [P, TT, E]
                        for j, c in enumerate((cw, cw2)):
                            link(dve.tensor_tensor(c[:, :, :], iot[:, :].unsqueeze(1).broadcast_to(wide),
                                                   idxf[:, :, j:j + 1].broadcast_to(wide), ALU.is_equal))
                            link(dve.tensor_tensor(c[:, :, :], c[:, :, :], wtop[:, :, j:j + 1].broadcast_to(wide), ALU.mult))
                        link(dve.tensor_tensor(cw[:, :, :], cw[:, :, :], cw2[:, :, :], ALU.add))
                        link(dve.tensor_copy(cc[:, :, 0:E], cw[:, :, :]))
                        dve.tensor_tensor(cc[:, :, E:2 * E], cw[:, :, :], cc[:, :, 0:E].bitcast(F32), ALU.subtract).then_inc(comb_ok, 1)
                        for _ in range(N_ROUTE - 4):
                            yield

                    def experts(b):
                        inst = n.before("experts")
                        for c in range(NCH + 2):
                            g = inst * NCH + c
                            k = g % 2
                            yield
                            if 1 <= c <= NCH:
                                dve.wait_ge(th_ok, g)
                                dve.tensor_tensor(tvl[:, 1 - k, :], tv[:, 1 - k, :], tvh[:, 1 - k, :].bitcast(F32),
                                                  ALU.subtract).then_inc(tl_ok, 1)
                            if c < NCH:
                                dve.wait_ge(tanh_ok, g + 1)
                                dve.scalar_tensor_tensor(out=th[:, k, :], in0=th[:, k, :], scalar=1.0, in1=Z[:, :],
                                                         op0=ALU.add, op1=ALU.mult).then_inc(z_used, 1)
                            yield
                            if c < NCH:
                                dve.wait_ge(z_used, g + 1)
                                if c < NROUTED:
                                    dve.wait_ge(c_full, n.next("c"))
                                    dve.tensor_tensor(tv[:, k, :], th[:, k, :], CWB[:, :], ALU.mult).then_inc(t_ok, 1)
                                else:
                                    dve.tensor_scalar(tv[:, k, :], th[:, k, :], 0.5, None, ALU.mult).then_inc(t_ok, 1)
                            yield

                    def finish(b):
                        dve.wait_ge(o_done, n.next("fin", NCH))
                        dve.tensor_copy(yT[:, 1, :], ACC[1][:, :]).then_inc(acc_out, 1)
                        yield
                        for j in range(2):
                            dve.wait_ge(fin_ps, n.next("fin_ps"))
                            rows = xs[:, b, 2 * j:2 * j + 2, :].rearrange("p t d -> p (t d)")
                            dve.tensor_tensor(rows, SC[j][:, :], rows, ALU.add).then_inc(x_upd, 1)
                            n.next("upd")
                            yield
                        yield

                    def half(b, hf):
                        def heads(ap):
                            return ap.rearrange("p (h d) -> p h d", d=HD)

                        def stack(t):
                            dve.wait_ge(raw_ok, n.n["raw"])
                            link(dve.tensor_tensor(heads(raw[:, t, :]), heads(raw[:, t, :]),
                                                   nrt[:, t, :].unsqueeze(2).broadcast_to([P, 3 * HH, HD]), ALU.mult))
                            k = n.n.get("stT", 0) + 2 * t
                            if k:
                                dve.wait_ge(stT_ps, k)
                            for st, first, step, c in ((stq, (0, 1), 2, 0), (stk, (0, 2), 1, HW)):
                                both = heads(raw[:, t, c:c + HW]).unsqueeze(2).broadcast_to([P, HH, 2, HD])
                                hi = st[:, :, first[0]:first[0] + step + 1:step, :]
                                lo = st[:, :, first[1]:first[1] + step + 1:step, :]
                                link(dve.tensor_copy(hi, both))
                                dve.tensor_tensor(lo, both, hi.bitcast(F32), ALU.subtract).then_inc(st_ok, 1)

                        n.next("raw", TT)
                        for step in range(N_PREP):
                            i = step - 1
                            if 0 <= i < TT:
                                dve.wait_ge(sq_ok, n.next("sq"))
                                dve.tensor_reduce(nrm[:, i, :], heads(sq[:, i % 2, :]), AX_X, ALU.add).then_inc(sq_used, 1)
                                dve.wait_ge(sq_used, n.next("sq_used"))
                                if i == TT - 1:
                                    link(dve.tensor_scalar(nry[:, :, :].bitcast(I32), nrm[:, :, :].bitcast(I32), 1, None,
                                                           ALU.arith_shift_right))
                                    link(dve.tensor_scalar(nry[:, :, :].bitcast(I32), nry[:, :, :].bitcast(I32), -1.0,
                                                           float(0x5F3759DF), ALU.mult, ALU.add))
                            elif TT <= i < TT + 4:
                                if i < TT + 3:
                                    link(dve.tensor_tensor(nrt[:, :, :], nry[:, :, :], nry[:, :, :], ALU.mult))
                                    link(dve.tensor_tensor(nrt[:, :, :], nrt[:, :, :], nrm[:, :, :], ALU.mult))
                                    link(dve.tensor_scalar(nrt[:, :, :], nrt[:, :, :], -0.5, 1.5, ALU.mult, ALU.add))
                                    link(dve.tensor_tensor(nry[:, :, :], nry[:, :, :], nrt[:, :, :], ALU.mult))
                                else:
                                    link(dve.tensor_tensor(nrt[:, :, :], nry[:, :, :], nrm[:, :, :], ALU.mult))
                                    link(dve.tensor_scalar(nrt[:, :, :], nrt[:, :, :], L2_EPS, None, ALU.add))
                                    link(dve.reciprocal(nrt[:, :, :], nrt[:, :, :]))
                                    link(dve.tensor_scalar(nrt[:, :, 0:HH], nrt[:, :, 0:HH], taub[:, 0:1], None, ALU.mult))
                            if TT + 4 <= i < 2 * TT + 4:
                                stack(i - TT - 4)
                            yield
                        n.next("stT", 2 * TT)
                        for u in range(NU + 4):
                            if 1 <= u <= NU:
                                qt, h = UNITS[u - 1]
                                k = (u - 1) % 2
                                dve.wait_ge(sc_ps, n.next("sc"))
                                dve.tensor_reduce(nmax[:, k:k + 1], SC[k][:, 0:(qt + 1) * P], AX_X, ALU.max,
                                                  negate=True).then_inc(max_ok, 1)
                            if 2 <= u < NU + 2:
                                qt, h = UNITS[u - 2]
                                k = n.next("pT")
                                if evacuates(u - 2) == "dve":
                                    dve.wait_ge(pT_ps, k)
                                    dve.tensor_copy(prT[:, u % 2, 0:(qt + 1) * P], TP[:, 0:(qt + 1) * P]).then_inc(pT_ok, 1)
                            if u >= 3 and u < NU + 3 and UNITS[u - 3][1] == HH - 1:
                                qt = UNITS[u - 3][0]
                                dve.wait_ge(p_ok, n.n.get("pv", 0) + u - 2)
                                link(dve.reciprocal(rden[:, :], den[:, qt % 2, :]))
                                link(dve.tensor_scalar(rden[:, :], rden[:, :], nub[:, 0:1], None, ALU.mult))
                                dve.wait_ge(pv_ps, n.n.get("pv", 0) + u - 2)
                                dve.tensor_tensor(heads(ov[:, :]), heads(OV[:, 0:HW]),
                                                  rden[:, :].unsqueeze(2).broadcast_to([P, HH, HD]), ALU.mult).then_inc(ov_free, 1)
                                dve.wait_ge(ov_free, n.next("ov"))
                                rows = xs[:, b, qt, hf * HW:(hf + 1) * HW]
                                dve.tensor_tensor(rows, rows, ov[:, :], ALU.add).then_inc(x_upd, 1)
                                n.next("upd")
                            yield
                        n.next("pv", NU)

                    round_of_two(norm, route, experts, finish, half)
            clear_all()


def kernel(**inputs):
    import concourse.bacc as _bacc
    from concourse.bass_utils import run_bass_kernel_spmd as _run

    a = {k: np.asarray(v) for k, v in inputs.items()}
    pre = "L0_attn_a_"
    mats_a = np.concatenate([a[pre + k] for k in ("w_y", "w_x", "w_ig", "w_ag", "w_out")], axis=1)
    q, k, v = (a["L0_attn_b_" + n].T for n in ("wq", "wk", "wv"))
    w_qkv = np.concatenate([m[:, hf * HW:(hf + 1) * HW] for hf in range(2) for m in (q, k, v)], axis=1)
    w1 = np.zeros((D, HID), np.float32)
    w1[:, 0:E * H] = a["L0_ffn_w1"].transpose(1, 0, 2).reshape(D, E * H)
    w1[:, E * H:(E + 1) * H] = a["L0_ffn_sw1"][0]
    w2 = np.zeros((HID, D), np.float32)
    w2[0:E * H] = a["L0_ffn_w2"].reshape(E * H, D)
    w2[E * H:(E + 1) * H] = a["L0_ffn_sw2"][0]
    rows = [a[pre + k] for k in ("b_y", "b_x", "conv_b", "a_param", "b_ig", "b_ag")] + list(a[pre + "conv_w"])
    vecs = np.stack(rows).reshape(NVEC, 2, P).transpose(2, 0, 1).reshape(P, NVEC * 2)
    sel = np.tile(np.repeat(np.eye(E, dtype=np.float32), H, axis=1), (2, 1))
    arrays = {
        "x": a[pre + "x"], "mats_a": mats_a, "w_qkv": w_qkv, "gate_w": a["L0_ffn_gate_w"].T, "w1": w1, "w2": w2,
        "vecs": vecs, "b_out": a[pre + "b_out"], "tau": a["L0_attn_b_tau"], "nu": a["L0_attn_b_nu"], "sel": sel,
    }
    arrays = {k: np.ascontiguousarray(v) for k, v in arrays.items()}
    nc = _bacc.Bacc("TRN2", target_bir_lowering=False, num_devices=1)
    args = [nc.dram_tensor(k, v.shape, mybir.dt.from_np(v.dtype), kind="ExternalInput").ap() for k, v in arrays.items()]
    out = nc.dram_tensor("out", (B, T, D), F32, kind="ExternalOutput").ap()
    hybrid_kernel(nc, *args, out)
    r = _run(nc, [arrays], core_ids=[0])
    return r.results[0]["out"]
```

```python
from contextlib import ExitStack

import concourse.bass as bass
import numpy as np
from concourse import mybir

ALU = mybir.AluOpType
ACT = mybir.ActivationFunctionType
F32 = mybir.dt.float32
F32R = mybir.dt.float32r
BF16 = mybir.dt.bfloat16
U32 = mybir.dt.uint32
I32 = mybir.dt.int32
AX_X = mybir.AxisListType.X

P = 128
B, T, D = 4, 512, 256
KD = D // P
TT = T // P
L = 256
TAPS = 4
E, H, TOPK = 16, 176, 2
G = 4
GS = E // G
NCH = -(-(E + 1) * H // P)
NROUTED = E * H // P
HID = NCH * P
assert E * H == NROUTED * P
HEADS, HD = 16, 16
HH = HEADS // 2
HP = HH // 2
HW = HH * HD
PAIR = 2
LN_EPS = 1e-5
L2_EPS = 1e-8
TOP_EPS = 1e-20
NEG = -1.0e30
NVEC = 10
(V_BY, V_BX, V_CB, V_AP, V_BIG, V_BAG, V_CW) = range(7)
MATS_A = 5
M_Y, M_X, M_IG, M_AG, M_OUT = range(MATS_A)


class Count:

    def __init__(self):
        self.n = {}

    def next(self, name, by=1):
        self.n[name] = self.n.get(name, 0) + by
        return self.n[name]

    def before(self, name):
        n = self.n.get(name, 0)
        self.n[name] = n + 1
        return n


def weave(main, n_main, side, weights):
    done, due = 0, 0.0
    for w in weights:
        next(side)
        due += w
        while done < round(due / sum(weights) * n_main):
            next(main)
            done += 1
    for rest in (main, side):
        assert next(rest, "end") == "end"


def hybrid_kernel(nc, x, mats_a, w_qkv, gate_w, w1, w2, vecs, b_out, tau, nu, sel, out):
    ctx = ExitStack()
    with ctx:
        def sb(name, shape, dt=F32, on=ctx):
            return on.enter_context(nc.sbuf_tensor(name, shape, dt))

        sems = []

        def sem(name):
            s = ctx.enter_context(nc.semaphore(name))
            sems.append(s)
            return s

        banks = [ctx.enter_context(nc.psum_tensor(f"bank{i}", [P, 512], F32)) for i in range(8)]

        w1h = sb("w1h", [P, KD, HID], F32R)
        w1l = sb("w1l", [P, KD, HID], F32R)
        w2h = sb("w2h", [P, NCH, D], F32R)
        w2l = sb("w2l", [P, NCH, D], F32R)
        gw = [sb(f"gw{i}", [P, KD, E], F32R) for i in range(2)]
        selr = sb("selr", [2 * E, NROUTED * P], F32R)
        xTh = [sb(f"xTh{b}", [P, KD, T], F32R) for b in range(PAIR)]
        xTl = [sb(f"xTl{b}", [P, KD, T], F32R) for b in range(PAIR)]
        ident = sb("ident", [P, P])
        identb = sb("identb", [P, P], BF16)
        maskb = sb("maskb", [P, P], BF16)
        maskTb = sb("maskTb", [P, P], BF16)
        mv = sb("mv", [P, PAIR, TT, 2])
        stats = sb("stats", [P, TT, 6])
        vare = sb("vare", [P, TT])
        rstd = sb("rstd", [P, PAIR, TT])
        mhalf = sb("mhalf", [P, TT])
        tri = sb("tri", [P, G, G])
        iot = sb("iot", [P, E])
        taub = sb("taub", [P, 1])
        nub = sb("nub", [P, 1])

        x_rows = x.rearrange("b (t p) d -> b p t d", p=P)
        out_rows = out.rearrange("b (t p) d -> b p t d", p=P)

        def clear():
            for s in sems:
                nc.sync.sem_clear(s)
            sems.clear()
            nc.all_engine_barrier()

        QA = B
        W1Q, W2Q = HID // QA, NCH // QA
        a_ctx = ExitStack()
        with a_ctx:
            def sba(name, shape, dt=F32):
                return sb(name, shape, dt, a_ctx)

            wa = [sba(f"wa{i}", [P, KD, MATS_A * L], F32R) for i in range(2)]
            vec = sba("vec", [P, NVEC * 2])
            cbx = sba("cbx", [P, 2])
            nsp = sba("nsp", [P, 2])
            sp1 = sba("sp1", [P, 2])
            sp2 = sba("sp2", [P, 2])
            one = sba("one", [P, 1])
            boutb = sba("boutb", [P, D])

            def v(which, m):
                return vec[:, 2 * which + m:2 * which + m + 1]

            p_ctx = ExitStack()
            with p_ctx:
                stage_a = sb("stage_a", [P, KD, MATS_A * L], F32, p_ctx)
                stage_s = sb("stage_s", [2 * E, NROUTED * P], F32, p_ctx)
                stage_g = sb("stage_g", [P, KD, E], F32, p_ctx)
                p_wa = [sem(f"p_wa{kk}") for kk in range(KD)]
                p_s, p_g, p_v, p_b, p_id, p_act, p_self, p_hi = (
                    sem(n) for n in ("p_s", "p_g", "p_v", "p_b", "p_id", "p_act", "p_self", "p_hi"))
                with nc.Block() as block:
                    @block.sync
                    def _(sp):
                        sp.dma_start(vec[:, :], vecs).then_inc(p_v, 16)
                        for kk in range(KD):
                            sp.dma_start(stage_a[:, kk, :], mats_a[kk * P:(kk + 1) * P, :]).then_inc(p_wa[kk], 16)
                        sp.dma_start(stage_s[:, :], sel).then_inc(p_s, 16)
                        for kk in range(KD):
                            sp.dma_start(stage_g[:, kk, :], gate_w[kk * P:(kk + 1) * P, :]).then_inc(p_g, 16)
                        sp.dma_start(boutb[:, :], b_out.rearrange("(o d) -> o d", o=1).broadcast_to([P, D])).then_inc(p_b, 16)
                        sp.dma_start(taub[:, :], tau.rearrange("(o d) -> o d", o=1).broadcast_to([P, 1])).then_inc(p_b, 16)
                        sp.dma_start(nub[:, :], nu.rearrange("(o d) -> o d", o=1).broadcast_to([P, 1])).then_inc(p_b, 16)
                        sp.wait_ge(p_b, 48)

                    @block.gpsimd
                    def _(pool):
                        pool.memset(ident[:, :], 0.0).then_inc(p_id, 1)
                        pool.memset(maskb[:, :], 0.0).then_inc(p_id, 1)
                        pool.memset(maskTb[:, :], 0.0).then_inc(p_id, 1)
                        pool.memset(mhalf[:, :], -0.5).then_inc(p_id, 1)
                        pool.memset(one[:, :], 1.0).then_inc(p_id, 1)
                        pool.wait_ge(p_id, 5)
                        pool.affine_select(out=ident[:, :], in_=ident[:, :], compare_op=ALU.not_equal, fill=1.0,
                                           base=0, pattern=[[-1, P]], channel_multiplier=1).then_inc(p_id, 1)
                        pool.affine_select(out=maskb[:, :], in_=maskb[:, :], compare_op=ALU.is_ge, fill=NEG,
                                           base=0, pattern=[[-1, P]], channel_multiplier=1).then_inc(p_id, 1)
                        pool.affine_select(out=maskTb[:, :], in_=maskTb[:, :], compare_op=ALU.is_ge, fill=NEG,
                                           base=0, pattern=[[1, P]], channel_multiplier=-1).then_inc(p_id, 1)
                        pool.wait_ge(p_id, 8)
                        pool.tensor_copy(identb[:, :], ident[:, :]).then_inc(p_id, 1)
                        pool.memset(tri[:, :, :], 1.0).then_inc(p_id, 1)
                        pool.iota(iot[:, :], pattern=[[1, E]], base=0, channel_multiplier=0,
                                  allow_small_or_imprecise_dtypes=True).then_inc(p_id, 1)
                        pool.wait_ge(p_id, 11)
                        pool.affine_select(out=tri[:, :, :], in_=tri[:, :, :], compare_op=ALU.is_gt, fill=0.0,
                                           base=0, pattern=[[1, G], [-1, G]], channel_multiplier=0).then_inc(p_id, 1)
                        pool.wait_ge(p_hi, 1)
                        pool.tensor_tensor(gw[1][:, :, :], stage_g[:, :, :], gw[0][:, :, :].bitcast(F32),
                                           ALU.subtract).then_inc(p_id, 1)

                    @block.scalar
                    def _(act):
                        act.wait_ge(p_v, 16)
                        act.activation(sp1[:, :], vec[:, 2 * V_AP:2 * V_AP + 2], ACT.Abs).then_inc(p_act, 1)
                        act.wait_ge(p_act, 1)
                        act.activation(sp2[:, :], sp1[:, :], ACT.Exp, scale=-1.0).then_inc(p_act, 1)
                        act.wait_ge(p_act, 2)
                        act.wait_ge(p_id, 5)
                        act.activation(sp1[:, :], sp2[:, :], ACT.Ln, bias=one[:, :]).then_inc(p_act, 1)
                        act.wait_ge(p_g, 16 * KD)
                        act.activation(gw[0][:, :, :], stage_g[:, :, :], ACT.Copy).then_inc(p_hi, 1)
                        act.wait_ge(p_s, 16)
                        act.activation(selr[:, :], stage_s[:, :], ACT.Copy).then_inc(p_hi, 1)

                    @block.vector
                    def _(dve):
                        dve.wait_ge(p_v, 16)
                        dve.tensor_tensor(cbx[:, :], vec[:, 2 * V_BX:2 * V_BX + 2],
                                          vec[:, 2 * (V_CW + TAPS - 1):2 * (V_CW + TAPS)], ALU.mult).then_inc(p_self, 1)
                        dve.wait_ge(p_self, 1)
                        dve.tensor_tensor(cbx[:, :], cbx[:, :], vec[:, 2 * V_CB:2 * V_CB + 2], ALU.add).then_inc(p_self, 1)
                        for kk in range(KD):
                            dve.wait_ge(p_wa[kk], 16)
                            dve.tensor_copy(wa[0][:, kk, :], stage_a[:, kk, :]).then_inc(p_self, 1)
                        for kk in range(KD):
                            dve.wait_ge(p_self, 3 + kk)
                            dve.tensor_tensor(wa[1][:, kk, :], stage_a[:, kk, :], wa[0][:, kk, :].bitcast(F32),
                                              ALU.subtract).then_inc(p_self, 1)
                        dve.wait_ge(p_act, 3)
                        dve.scalar_tensor_tensor(out=nsp[:, :], in0=vec[:, 2 * V_AP:2 * V_AP + 2], scalar=0.0,
                                                 in1=sp1[:, :], op0=ALU.max, op1=ALU.add).then_inc(p_self, 1)
                        dve.wait_ge(p_self, 2 * KD + 3)
                        dve.tensor_scalar(nsp[:, :], nsp[:, :], -8.0, None, ALU.mult).then_inc(p_self, 1)
                clear()

            def pair(name, shape, dt=F32):
                return [sba(f"{name}{b}", shape, dt) for b in range(PAIR)]

            xs = pair("xs_a", [P, TT, D])
            xb = pair("xb", [P, 2, TAPS - 1 + T])
            cv = pair("cv", [P, 2, T])
            gx = pair("gx", [P, 2, T])
            av = pair("av", [P, 2, T])
            yv = pair("yv", [P, 2, T])
            st1 = sba("st1", [P, KD, W1Q])
            st2 = sba("st2", [P, W2Q, D])
            xn = [a_[:, :, :].rearrange("p m t -> p (m t)").rearrange("p (t d) -> p t d", t=TT) for a_ in av]
            sh, sl = xTh, xTl

            a_x = [sem(f"a_x{b}") for b in range(PAIR)]
            (a_w1, a_w2, a_out, a_bn, a_ln, a_rstd, a_xn, a_tp, a_hi, a_lo, a_ps, a_xb, a_y, a_conv, a_chi,
             a_clo, a_gate, a_g, a_e, a_na, a_m, a_hy, a_hyh, a_hyl, a_o, a_xr, a_wh, a_wl, a_self, a_pool,
             a_xsum, a_conv_step, a_gm, a_scan) = (
                sem(n) for n in (
                    "a_w1", "a_w2", "a_out", "a_bn", "a_ln", "a_rstd", "a_xn", "a_tp", "a_hi", "a_lo", "a_ps",
                    "a_xb", "a_y", "a_conv", "a_chi", "a_clo", "a_gate", "a_g", "a_e", "a_na", "a_m", "a_hy",
                    "a_hyh", "a_hyl", "a_o", "a_xr", "a_wh", "a_wl", "a_self", "a_pool", "a_xsum",
                    "a_conv_step", "a_gm", "a_scan"))

            bTY = [banks[2 * b:2 * b + 2] for b in range(PAIR)]
            bXB = [banks[4 + 2 * b:6 + 2 * b] for b in range(PAIR)]
            bG = [banks[4:8], banks[0:4]]
            CH = [(b, m) for b in range(PAIR) for m in range(2)]
            with nc.Fori(0, B // PAIR) as it:
                with nc.Block() as block:
                    @block.sync
                    def _(sp):
                        for b in range(PAIR):
                            sp.dma_start(xs[b][:, :, :], x_rows[bass.ds(it * PAIR + b, 1), :, :, :]
                                         .rearrange("o p t d -> (o p) t d")).then_inc(a_x[b], 16)
                        for q in range(QA // PAIR):
                            part = it * (QA // PAIR) + q
                            if q:
                                sp.wait_ge(a_wl, 2 * q - 1)
                            for kk in range(KD):
                                sp.dma_start(st1[:, kk, :], w1[kk * P:(kk + 1) * P, bass.ds(part * W1Q, W1Q)]).then_inc(a_w1, 16)
                            if q:
                                sp.wait_ge(a_wl, 2 * q)
                            sp.dma_start(st2[:, :, :], w2.rearrange("(q c p) d -> q p c d", p=P, q=QA)[bass.ds(part, 1), :, :, :]
                                         .rearrange("o p c d -> (o p) c d")).then_inc(a_w2, 16)
                        for b in range(PAIR):
                            sp.wait_ge(a_xsum, 2 * (b + 1))
                            sp.dma_start(out_rows[bass.ds(it * PAIR + b, 1), :, :, :].rearrange("o p t d -> (o p) t d"),
                                         xs[b][:, :, :]).then_inc(a_out, 16)
                        sp.wait_ge(a_out, 16 * PAIR)

                    @block.gpsimd
                    def _(pool):
                        for b in range(PAIR):
                            pool.wait_ge(a_ln, TT * (b + 1))
                            if b:
                                pool.wait_ge(a_rstd, b)
                            pool.tensor_scalar(vare[:, :], mv[:, b, :, 1], LN_EPS, None, ALU.add).then_inc(a_pool, 1)
                            pool.wait_ge(a_pool, b + 1)
                            pool.tensor_tensor(rstd[:, b, :], vare[:, :], mhalf[:, :], ALU.pow).then_inc(a_rstd, 1)
                        for b in range(PAIR):
                            pool.wait_ge(a_xn, TT * (b + 1))
                            for t in range(TT):
                                pool.tensor_tensor(xs[b][:, t, :], xs[b][:, t, :], boutb[:, :], ALU.add).then_inc(a_xr, 1)
                        for q in range(QA // PAIR):
                            part = it * (QA // PAIR) + q
                            pool.wait_ge(a_wh, 2 * q + 1)
                            pool.tensor_tensor(w1l[:, :, bass.ds(part * W1Q, W1Q)], st1[:, :, :],
                                               w1h[:, :, bass.ds(part * W1Q, W1Q)].bitcast(F32), ALU.subtract).then_inc(a_wl, 1)
                            pool.wait_ge(a_wh, 2 * q + 2)
                            pool.tensor_tensor(w2l[:, bass.ds(part * W2Q, W2Q), :], st2[:, :, :],
                                               w2h[:, bass.ds(part * W2Q, W2Q), :].bitcast(F32), ALU.subtract).then_inc(a_wl, 1)

                    @block.scalar
                    def _(act):
                        def high_w1(q):
                            part = it * (QA // PAIR) + q
                            act.wait_ge(a_w1, 16 * KD * (q + 1))
                            act.activation(w1h[:, :, bass.ds(part * W1Q, W1Q)], st1[:, :, :], ACT.Copy).then_inc(a_wh, 1)

                        def high_w2(q):
                            part = it * (QA // PAIR) + q
                            act.wait_ge(a_w2, 16 * (q + 1))
                            act.activation(w2h[:, bass.ds(part * W2Q, W2Q), :], st2[:, :, :], ACT.Copy).then_inc(a_wh, 1)

                        for i, (b, kk) in enumerate(CH):
                            act.wait_ge(a_tp, i + 1)
                            act.activation(xTh[b][:, kk, :], bTY[b][kk][:, :], ACT.Copy).then_inc(a_hi, 1)
                        high_w1(0)
                        for i, (b, m) in enumerate(CH):
                            act.wait_ge(a_ps, i + 1)
                            act.activation(cv[b][:, m, :], bXB[b][m][:, :], ACT.Identity, bias=cbx[:, m:m + 1],
                                           scale=v(V_CW + TAPS - 1, m))
                            act.activation(xb[b][:, m, TAPS - 1:], bXB[b][m][:, :], ACT.Identity, bias=v(V_BX, m)).then_inc(a_xb, 1)
                        act.wait_ge(a_ps, 6)
                        for m in range(2):
                            act.wait_ge(a_conv, m + 1)
                            act.activation(sh[0][:, m, :], cv[0][:, m, :], ACT.Copy).then_inc(a_chi, 1)
                        for i, (b, m) in enumerate(CH):
                            act.wait_ge(a_ps, i + 5)
                            act.activation(yv[b][:, m, :], bTY[b][m][:, :], ACT.Gelu, bias=v(V_BY, m)).then_inc(a_y, 1)
                        for m in range(2):
                            act.wait_ge(a_conv, m + 3)
                            act.activation(sh[1][:, m, :], cv[1][:, m, :], ACT.Copy).then_inc(a_chi, 1)
                        high_w2(0)
                        for j in range(8):
                            b, gate, m = j // 4, j // 2 % 2, j % 2
                            dst, bias = ((gx, V_BIG), (av, V_BAG))[gate]
                            act.wait_ge(a_gate, j + 1)
                            act.activation(dst[b][:, m, :], bG[b][2 * gate + m][:, :], ACT.Sigmoid, bias=v(bias, m)).then_inc(a_g, 1)
                        for b, m in CH:
                            act.wait_ge(a_g, 4 * b + m + 3)
                            act.activation(av[b][:, m, :], av[b][:, m, :], ACT.Exp, scale=nsp[:, m:m + 1]).then_inc(a_e, 1)
                        for i, (b, m) in enumerate(CH):
                            act.wait_ge(a_na, i + 1)
                            act.activation(xb[b][:, m, TAPS - 1:], xb[b][:, m, TAPS - 1:], ACT.Sqrt, bias=one[:, :]).then_inc(a_m, 1)
                        for i, (b, m) in enumerate(CH):
                            if i == 2:
                                high_w1(1)
                            act.wait_ge(a_hy, i + 1)
                            act.activation(sh[b][:, m, :], yv[b][:, m, :], ACT.Copy).then_inc(a_hyh, 1)
                        high_w2(1)

                    @block.vector
                    def _(dve):
                        n = Count()

                        def link(ins):
                            ins.then_inc(a_self, 1)
                            dve.wait_ge(a_self, n.next("self"))

                        for b in range(PAIR):
                            dve.memset(xb[b][:, :, 0:TAPS - 1], 0.0).then_inc(a_self, 1)
                            n.next("self")
                        for b in range(PAIR):
                            dve.wait_ge(a_x[b], 16)
                            for t in range(TT):
                                dve.bn_stats(stats[:, t, :], xs[b][:, t, :]).then_inc(a_bn, 1)
                            for t in range(TT):
                                dve.wait_ge(a_bn, TT * b + t + 1)
                                last = dve.bn_aggr(mv[:, b, t, :], stats[:, t, :]).then_inc(a_ln, 1)
                            dve.wait_ge(a_ln, TT * (b + 1))
                        for b in range(PAIR):
                            dve.wait_ge(a_rstd, b + 1)
                            for t in range(TT):
                                dve.tensor_scalar(xn[b][:, t, :], xs[b][:, t, :], mv[:, b, t, 0:1], rstd[:, b, t:t + 1],
                                                  ALU.subtract, ALU.mult).then_inc(a_xn, 1)
                        for i, (b, kk) in enumerate(CH):
                            dve.wait_ge(a_hi, i + 1)
                            dve.tensor_tensor(xTl[b][:, kk, :], bTY[b][kk][:, :], xTh[b][:, kk, :].bitcast(F32),
                                              ALU.subtract).then_inc(a_lo, 1)

                        def low_conv(m):
                            dve.wait_ge(a_chi, m + 1)
                            dve.tensor_tensor(sl[0][:, m, :], cv[0][:, m, :], sh[0][:, m, :].bitcast(F32), ALU.subtract).then_inc(a_clo, 1)

                        for b in range(PAIR):
                            for k in range(TAPS - 1):
                                for m in range(2):
                                    if k == 0:
                                        dve.wait_ge(a_xb, 2 * b + m + 1)
                                    if k:
                                        dve.wait_ge(a_conv_step, 4 * b + 2 * k + m - 1)
                                    dve.scalar_tensor_tensor(
                                        out=cv[b][:, m, :], in0=xb[b][:, m, k:k + T], scalar=v(V_CW + k, m), in1=cv[b][:, m, :],
                                        op0=ALU.mult, op1=ALU.add).then_inc(a_conv_step if k < TAPS - 2 else a_conv, 1)
                                if b and k < 2:
                                    low_conv(k)
                        for m in range(2):
                            dve.wait_ge(a_chi, m + 3)
                            dve.tensor_tensor(sl[1][:, m, :], cv[1][:, m, :], sh[1][:, m, :].bitcast(F32), ALU.subtract).then_inc(a_clo, 1)
                        for b, m in CH:
                            dve.wait_ge(a_g, 4 * b + m + 1)
                            last = dve.tensor_tensor(gx[b][:, m, :], gx[b][:, m, :], cv[b][:, m, :], ALU.mult)
                        link(last)
                        for i, (b, m) in enumerate(CH):
                            dve.wait_ge(a_e, i + 1)
                            link(dve.memset(av[b][:, m, 0:1], 0.0))
                            dve.scalar_tensor_tensor(out=xb[b][:, m, TAPS - 1:], in0=av[b][:, m, :], scalar=-1.0,
                                                     in1=av[b][:, m, :], op0=ALU.mult, op1=ALU.mult).then_inc(a_na, 1)
                        def low_hy(b):
                            for m in range(2):
                                dve.wait_ge(a_hyh, 2 * b + m + 1)
                                dve.tensor_tensor(sl[b][:, m, :], yv[b][:, m, :], sh[b][:, m, :].bitcast(F32), ALU.subtract).then_inc(a_hyl, 1)

                        for b in range(PAIR):
                            for m in range(2):
                                dve.wait_ge(a_m, 2 * b + m + 1)
                                dve.tensor_tensor(gx[b][:, m, :], gx[b][:, m, :], xb[b][:, m, TAPS - 1:], ALU.mult).then_inc(a_gm, 1)
                            if b:
                                low_hy(0)
                            for m in range(2):
                                dve.wait_ge(a_gm, 2 * b + m + 1)
                                dve.tensor_tensor_scan(cv[b][:, m, :], av[b][:, m, :], gx[b][:, m, :], 0.0, ALU.mult, ALU.add).then_inc(a_scan, 1)
                            for m in range(2):
                                dve.wait_ge(a_scan, 2 * b + m + 1)
                                dve.wait_ge(a_y, 2 * b + m + 1)
                                dve.tensor_tensor(yv[b][:, m, :], cv[b][:, m, :], yv[b][:, m, :], ALU.mult).then_inc(a_hy, 1)
                        low_hy(1)
                        for b in range(PAIR):
                            for j in range(2):
                                dve.wait_ge(a_xr, TT * b + 2 * j + 2)
                                dve.wait_ge(a_o, 2 * b + j + 1)
                                rows = xs[b][:, 2 * j:2 * j + 2, :].rearrange("p t d -> p (t d)")
                                dve.tensor_tensor(rows, bXB[b][j][:, :], rows, ALU.add).then_inc(a_xsum, 1)

                    @block.tensor
                    def _(pe):
                        for b in range(PAIR):
                            pe.wait_ge(a_xn, TT * (b + 1))
                            for kk in range(KD):
                                for t in range(TT):
                                    last = pe.transpose(bTY[b][kk][:, t * P:(t + 1) * P], xn[b][:, t, kk * P:(kk + 1) * P], ident[:, :])
                                last.then_inc(a_tp, 1)

                        def product(bank, mat, m, hi, lo):
                            for kk in range(KD):
                                w = [wa[i][:, kk, mat * L + m * P:mat * L + (m + 1) * P] for i in range(2)]
                                pe.matmul(bank, w[0], hi[:, kk, :], start=(kk == 0), stop=False)
                                pe.matmul(bank, w[1], hi[:, kk, :], start=False, stop=False)
                                last = pe.matmul(bank, w[0], lo[:, kk, :], start=False, stop=(kk == KD - 1))
                            return last

                        for b in range(PAIR):
                            pe.wait_ge(a_lo, KD * (b + 1))
                            for m in range(2):
                                product(bXB[b][m][:, :], M_X, m, xTh[b], xTl[b]).then_inc(a_ps, 1)
                        for b in range(PAIR):
                            for m in range(2):
                                product(bTY[b][m][:, :], M_Y, m, xTh[b], xTl[b]).then_inc(a_ps, 1)
                        for b in range(PAIR):
                            pe.wait_ge(a_clo, 2 * (b + 1))
                            for j in range(4):
                                if j % 2 == 0 and (b, j) != (0, 0):
                                    if b == 0:
                                        pe.wait_ge(a_xb, 4)
                                    else:
                                        pe.wait_ge(a_y, 2 + j)
                                product(bG[b][j][:, :], (M_IG, M_AG)[j // 2], j % 2, sh[b], sl[b]).then_inc(a_gate, 1)
                        for b in range(PAIR):
                            pe.wait_ge(a_hyl, 2 * (b + 1))
                            for t in range(TT):
                                rows = bXB[b][t // 2][:, t % 2 * D:(t % 2 + 1) * D]
                                for kk in range(KD):
                                    w = [wa[i][:, kk, M_OUT * L:(M_OUT + 1) * L] for i in range(2)]
                                    tok = slice(t * P, (t + 1) * P)
                                    pe.matmul(rows, sh[b][:, kk, tok], w[0], start=(kk == 0), stop=False)
                                    pe.matmul(rows, sh[b][:, kk, tok], w[1], start=False, stop=False)
                                    last = pe.matmul(rows, sl[b][:, kk, tok], w[0], start=False, stop=(kk == KD - 1))
                                if t % 2:
                                    last.then_inc(a_o, 1)
                clear()

        Z, CWB, ACC, SC, TP, OV = banks[0], banks[1], banks[2:4], banks[4:6], banks[6], banks[7]
        MX = (SC[0], SC[1], OV)

        wqkv = [sb(f"wqkv{i}", [P, KD, 3 * D], F32R) for i in range(2)]
        xs = sb("xs", [P, PAIR, TT, D])
        big = sb("big", [P, TT * D])
        xn = big[:, :].rearrange("p (t d) -> p t d", t=TT)
        yT = big[:, :].rearrange("p (m t) -> p m t", m=KD)
        spare = big[:, TT * D // 2:]
        pmx, pmn = (spare[:, i * TT * G * 2:(i + 1) * TT * G * 2].rearrange("p (t g e) -> p t g e", t=TT, g=G) for i in range(2))
        gcmp, gcm2 = (spare[:, (i + 1) * TT * G * G:(i + 2) * TT * G * G].rearrange("p (t g e) -> p t g e", t=TT, g=G) for i in range(2))
        cw, cw2 = (spare[:, (i + 3) * TT * E:(i + 4) * TT * E].rearrange("p (t e) -> p t e", t=TT) for i in range(2))
        VC = 2 * HD
        vx = big[:, :].rearrange("p (t h c) -> p t h c", t=TT, h=HH)
        th = sb("th", [P, 2, T])
        tv = sb("tv", [P, 2, T])
        tvh = sb("tvh", [P, 2, T], F32R)
        tvl = sb("tvl", [P, 2, T], F32R)
        cT = [sb(f"cT{b}", [2 * E, T], F32R) for b in range(PAIR)]
        score = sb("score", [P, TT, G, GS])
        gsum = sb("gsum", [P, TT, G])
        gbest = sb("gbest", [P, TT, G])
        top8 = sb("top8", [P, TT, 8])
        idx8 = sb("idx8", [P, TT, 8], U32)
        idxf = sb("idxf", [P, TT, TOPK])
        wsum = sb("wsum", [P, TT])
        wtop = sb("wtop", [P, TT, TOPK])
        cc = sb("cc", [P, TT, 2 * E], F32R)
        raw = sb("raw", [P, TT, 3 * HW])
        nrm = sb("nrm", [P, TT, 3 * HH])
        nrt = sb("nrt", [P, TT, 3 * HH])
        nry = sb("nry", [P, TT, 3 * HH])
        oT = raw[:, :, :].rearrange("p t c -> p (t c)")[:, 0:2 * T].rearrange("p (g q) -> p g q", g=2)
        stq = sb("stq", [P, TT, HH, 4, HD], F32R)
        qT = sb("qT", [P, HP, T], F32R)
        kT = sb("kT", [P, HP, T], F32R)
        pr = sb("pr", [P, 2, T])
        sq = pr[:, :, 0:3 * HW]
        stage_q = raw[:, :, :].rearrange("p t c -> p (t c)").rearrange("p (k c) -> p k c", k=KD)
        stk = [pr[:, i, :].bitcast(F32R).rearrange("p (h f d) -> p h f d", h=HH, f=4) for i in range(2)]
        HI_OF, LO_OF = (slice(0, 3, 2), slice(0, 2)), (slice(1, 2), slice(2, 3))
        osum = pr[:, :, 0:TT * HW // 2]
        rden = sb("rden", [P, 2, TT, HH // 2])

        UNITS = [(qt, h, max(1, TT // (qt + 1))) for qt in range(TT) for h in range(0, HH, max(1, TT // (qt + 1)))]
        NU = len(UNITS)
        LAST = [max(u for u in range(NU) if UNITS[u][0] == qt) for qt in range(TT)]
        ORDER = list(range(0, HH, 2)) + list(range(1, HH, 2))
        PUNITS = [(h, js) for h in range(HH) for js in ((0,), (1,), (2, 3))]
        NP = len(PUNITS)
        HG = HH // 2
        N_EXPERTS = 3 * (NCH + 2)
        W_NORM = [3.3, 2.0, 0.8, 0.7, 1.5, 0.0]
        W_ROUTE = [1.6] * 5 + [1.0, 1.0, 0.0]
        W_FIN = [2.0, 1.0, 1.0, 1.0]
        W_PREP = [0.2] * TT + [2.5] * 5 + [1.5] * (TT + 1)
        W_MAX = [0.3] * (NU + 2)
        W_PROB = [0.75] + [0.4] * (NP - 1) + [1.2] * 5
        N_NORM, N_ROUTE, N_FIN, N_PREP = (len(w) for w in (W_NORM, W_ROUTE, W_FIN, W_PREP))
        X_EXPERTS, X_ATTENTION = 2, 4

        x_in = [sem(f"x_in{b}") for b in range(PAIR)]
        (q_in, q_hi, q_lo, x_out, self_dve, self_pool, ln_stats, rstd_ok, xn_ok, xt_ps, xt_hi, xt_lo, rt_ps,
         rt_exp, comb_ok, ct_ps, ct_ok, z_full, u_ok, z_used, c_full, t_ok, th_ok, tl_ok, o_done, acc_out,
         fin_ps, x_upd, qkv_ps, sq_ok, raw_ok, sq_used, st_ok, stT_ps, qT_ok, kT_ok, sc_ps,
         max_ok, p_ok, mul_ok, sthi_ok, guess_ok, rs_ok, q2_ps, q2_ok, vx_ok, pT_ps, pv_ps, oT_ok, o_ps) = (
            sem(name) for name in (
                "q_in", "q_hi", "q_lo", "x_out", "self_dve", "self_pool", "ln_stats", "rstd_ok", "xn_ok",
                "xt_ps", "xt_hi", "xt_lo", "rt_ps", "rt_exp", "comb_ok", "ct_ps", "ct_ok", "z_full", "u_ok",
                "z_used", "c_full", "t_ok", "th_ok", "tl_ok", "o_done", "acc_out", "fin_ps", "x_upd", "qkv_ps",
                "sq_ok", "raw_ok", "sq_used", "st_ok", "stT_ps", "qT_ok", "kT_ok", "sc_ps",
                "max_ok", "p_ok", "mul_ok", "sthi_ok", "guess_ok", "rs_ok", "q2_ps", "q2_ok", "vx_ok", "pT_ps", "pv_ps",
                "oT_ok", "o_ps"))

        def round_of_two(norm, route, experts, finish, half, weights_qkv=None):
            def attention(b):
                yield from finish(b)
                yield from norm(b)
                yield from half(b, 0)
                yield from half(b, 1)
                yield from norm(b)
                yield from route(b)

            def both(first, then):
                yield from first
                yield from then

            def norm_route(b):
                yield from norm(b)
                yield from route(b)

            w_attention = W_FIN + W_NORM + 2 * (W_PREP + W_MAX + W_PROB) + [1.5 * w for w in W_NORM + W_ROUTE]
            for _ in norm(0):
                pass
            if weights_qkv is not None:
                weights_qkv()
            weave(experts(0), N_EXPERTS, both(route(0), norm_route(1)), [0.5] + [0.0] * (N_ROUTE - 1) + W_NORM + W_ROUTE)
            weave(experts(1), N_EXPERTS, attention(0), w_attention)
            weave(experts(0), N_EXPERTS, attention(1), w_attention)
            weave(experts(1), N_EXPERTS, finish(0), W_FIN)
            for _ in finish(1):
                pass

        with nc.Fori(0, B // PAIR) as it:
            with nc.Block() as block:
                @block.sync
                def _(sp):
                    for b in range(PAIR):
                        sp.dma_start(xs[:, b, :, :], out_rows[bass.ds(it * PAIR + b, 1), :, :, :]
                                     .rearrange("o p t d -> (o p) t d")).then_inc(x_in[b], 16)
                    for kk in range(KD):
                        sp.dma_start(stage_q[:, kk, :], w_qkv[kk * P:(kk + 1) * P, :]).then_inc(q_in, 16)
                    for b in range(PAIR):
                        sp.wait_ge(x_upd, PAIR * (X_EXPERTS + X_ATTENTION) + (b + 1) * X_EXPERTS)
                        sp.dma_start(out_rows[bass.ds(it * PAIR + b, 1), :, :, :].rearrange("o p t d -> (o p) t d"),
                                     xs[:, b, :, :]).then_inc(x_out, 16)
                    sp.wait_ge(x_out, 16 * PAIR)

                @block.tensor
                def _(pe):
                    n = Count()

                    def split_product(o, a, b, start, stop):
                        pe.matmul(o, a[0], b[0], start=start, stop=False)
                        pe.matmul(o, a[1], b[0], start=False, stop=False)
                        return pe.matmul(o, a[0], b[1], start=False, stop=stop)

                    def norm(b):
                        for _ in range(3):
                            yield
                        pe.wait_ge(xn_ok, n.next("xn", TT))
                        for kk in range(KD):
                            for t in range(TT):
                                last = pe.transpose(SC[kk][:, t * P:(t + 1) * P], xn[:, t, kk * P:(kk + 1) * P], ident[:, :])
                            last.then_inc(xt_ps, 1)
                            yield
                        pe.wait_ge(xt_lo, n.next("xt_lo", KD))
                        yield

                    def route(b):
                        for t in range(TT):
                            tok = slice(t * P, (t + 1) * P)
                            for kk in range(KD):
                                last = split_product(TP[:, t * E:(t + 1) * E], (xTh[b][:, kk, tok], xTl[b][:, kk, tok]),
                                                     (gw[0][:, kk, :], gw[1][:, kk, :]), kk == 0, kk == KD - 1)
                        last.then_inc(rt_ps, 1)
                        for _ in range(N_ROUTE - 2):
                            yield
                        pe.wait_ge(comb_ok, n.next("comb"))
                        for t in range(TT):
                            last = pe.transpose(TP[0:2 * E, t * P:(t + 1) * P], cc[:, t, :].bitcast(F32), ident[:, :])
                        last.then_inc(ct_ps, 1)
                        yield
                        yield

                    def experts(b):
                        inst = n.before("experts")
                        for c in range(NCH + 2):
                            g = inst * NCH + c
                            if c < NCH:
                                hid = slice(c * P, (c + 1) * P)
                                if g:
                                    pe.wait_ge(z_used, g)
                                for kk in range(KD):
                                    last = split_product(Z[:, :], (w1h[:, kk, hid], w1l[:, kk, hid]),
                                                         (xTh[b][:, kk, :], xTl[b][:, kk, :]), kk == 0, kk == KD - 1)
                                last.then_inc(z_full, 1)
                            yield
                            if c >= 2:
                                if c == 2 and inst:
                                    pe.wait_ge(acc_out, KD * inst)
                                pe.wait_ge(tl_ok, g - 1)
                            for m in range(KD):
                                if m == 1 and c < NROUTED:
                                    if c == 0:
                                        pe.wait_ge(ct_ok, n.next("ct"))
                                    if g:
                                        pe.wait_ge(t_ok, g)
                                    pe.matmul(CWB[:, :], selr[:, c * P:(c + 1) * P], cT[b][:, :], start=True, stop=True).then_inc(c_full, 1)
                                if c >= 2:
                                    k = g % 2
                                    last = split_product(ACC[m][:, :], (w2h[:, c - 2, m * P:(m + 1) * P], w2l[:, c - 2, m * P:(m + 1) * P]),
                                                         (tvh[:, k, :], tvl[:, k, :]), c == 2, c == NCH + 1)
                                    if m == KD - 1:
                                        last.then_inc(o_done, 1)
                                yield

                    def finish(b):
                        yield
                        pe.wait_ge(acc_out, n.next("acc", KD))
                        for j in range(2):
                            for t in range(2):
                                for kk in range(KD):
                                    last = pe.transpose(SC[j][:, t * D + kk * P:t * D + (kk + 1) * P],
                                                        yT[:, kk, (2 * j + t) * P:(2 * j + t + 1) * P], ident[:, :])
                            last.then_inc(fin_ps, 1)
                            n.next("upd")
                            yield
                        yield

                    def half(b, hf):
                        cols = slice(hf * 3 * HW, (hf + 1) * 3 * HW)
                        pe.wait_ge(x_upd, n.n["upd"])
                        if n.before("halves") == 0:
                            pe.wait_ge(q_lo, 2)
                        for i in range(N_PREP):
                            if i < TT:
                                t = i
                                if t >= 2:
                                    pe.wait_ge(raw_ok, n.n.get("raw", 0) + t - 1)
                                tok = slice(t * P, (t + 1) * P)
                                for kk in range(KD):
                                    last = split_product(SC[t % 2][:, 0:3 * HW], (xTh[b][:, kk, tok], xTl[b][:, kk, tok]),
                                                         (wqkv[0][:, kk, cols], wqkv[1][:, kk, cols]), kk == 0, kk == KD - 1)
                                last.then_inc(qkv_ps, 1)
                            if i == TT:
                                n.next("raw", TT)
                            if i >= TT + 6:
                                t = i - TT - 6
                                pe.wait_ge(st_ok, n.next("st", 2))
                                k = n.n.get("qkT", 0) + t
                                for bank, st, free in ((TP, stq[:, t, :, :, :], qT_ok), (OV, stk[t % 2], kT_ok)):
                                    if k:
                                        pe.wait_ge(free, k)
                                    rows = st.bitcast(F32).rearrange("p (j h) f d -> p j (h f d)", h=2)
                                    for j in range(HP):
                                        last = pe.transpose(bank[:, j * P:(j + 1) * P], rows[:, j, :], ident[:, :])
                                    last.then_inc(stT_ps, 1)
                            yield
                        for ready in (qT_ok, kT_ok):
                            pe.wait_ge(ready, n.n.get("qkT", 0) + TT)
                        n.next("qkT", TT)
                        before = n.n.get("max", 0)
                        for u in range(NU + 2):
                            if u < NU:
                                if u >= 3:
                                    pe.wait_ge(max_ok, before + u - 2)
                                qt, h0, nh = UNITS[u]
                                w = (qt + 1) * P
                                for j in range(nh):
                                    h = ORDER[h0 + j]
                                    r = slice((h % 2) * 64, (h % 2) * 64 + 64)
                                    pe.matmul(MX[u % 3][:, j * w:(j + 1) * w], qT[r, h // 2, qt * P:(qt + 1) * P],
                                              kT[r, h // 2, 0:w], start=True, stop=False)
                                    last = pe.matmul(MX[u % 3][:, (j + 1) * w - P:(j + 1) * w], identb[:, :], maskb[:, :],
                                                     start=False, stop=True)
                                last.then_inc(sc_ps, 1)
                            if u - 2 in LAST:
                                t = LAST.index(u - 2)
                                pe.wait_ge(max_ok, before + u - 1)
                                if t:
                                    pe.wait_ge(q2_ok, n.n.get("q2", 0) + t)
                                rows = stq[:, t, :, :, :].bitcast(F32).rearrange("p (j h) f d -> p j (h f d)", h=2)
                                for j in range(HP):
                                    last = pe.transpose(TP[:, j * P:(j + 1) * P], rows[:, j, :], ident[:, :])
                                last.then_inc(q2_ps, 1)
                            yield
                        n.next("max", NU)
                        for v in range(NP + 5):
                            if v == 0:
                                pe.wait_ge(q2_ok, n.next("q2", TT))
                                if hf == 0:
                                    pe.wait_ge(vx_ok, n.next("vx", 2))
                            if 2 <= v < NP + 2:
                                h, js = PUNITS[v - 2]
                                pe.wait_ge(p_ok, n.n.get("p", 0) + v - 1)
                                c = 0
                                for j in js:
                                    w = T - j * P
                                    g, i = h // HG, h % HG
                                    last = pe.matmul((TP, OV)[g][i * VC:(i + 1) * VC, j * P:], vx[:, j, h, :],
                                                     pr[:, v % 2, c:c + w], start=(j == 0), stop=(j == TT - 1),
                                                     tile_position=(0, i * VC))
                                    c += w
                                last.then_inc(pv_ps, 1)
                            if v < NP:
                                h, js = PUNITS[v]
                                r = slice((h % 2) * 64, (h % 2) * 64 + 64)
                                c = 0
                                for j in js:
                                    w = T - j * P
                                    pe.matmul(SC[v % 2][:, c:c + w], kT[r, h // 2, j * P:(j + 1) * P], qT[r, h // 2, j * P:],
                                              start=True, stop=False)
                                    last = pe.matmul(SC[v % 2][:, c:c + P], identb[:, :], maskTb[:, :], start=False, stop=True)
                                    c += w
                                last.then_inc(pT_ps, 1)
                            if NP + 2 <= v < NP + 4:
                                g = v - NP - 2
                                pe.wait_ge(oT_ok, n.next("oT"))
                                for t in range(TT):
                                    last = pe.transpose(SC[g][:, t * P:(t + 1) * P], oT[:, g, t * P:(t + 1) * P], ident[:, :])
                                last.then_inc(o_ps, 1)
                                n.next("upd")
                            yield
                        n.next("p", NP)

                    round_of_two(norm, route, experts, finish, half)

                @block.scalar
                def _(act):
                    n = Count()

                    def norm(b):
                        for _ in range(3):
                            yield
                        for kk in range(KD):
                            act.wait_ge(xt_ps, n.next("xt"))
                            act.activation(xTh[b][:, kk, :], SC[kk][:, :], ACT.Copy).then_inc(xt_hi, 1)
                            yield
                        yield

                    def route(b):
                        act.wait_ge(rt_ps, n.next("rt"))
                        act.activation(score[:, :, :, :].rearrange("p t g e -> p (t g e)"), TP[:, 0:TT * E], ACT.Exp,
                                       scale=-1.0).then_inc(rt_exp, 1)
                        for _ in range(N_ROUTE - 2):
                            yield
                        act.wait_ge(ct_ps, n.next("ct"))
                        act.activation(cT[b][:, :], TP[0:2 * E, :], ACT.Copy).then_inc(ct_ok, 1)
                        yield
                        yield

                    def experts(b):
                        inst = n.before("experts")
                        for c in range(NCH + 2):
                            g = inst * NCH + c
                            yield
                            if c < NCH:
                                k = g % 2
                                if g >= 2:
                                    act.wait_ge(t_ok, g - 1)
                                act.wait_ge(z_full, g + 1)
                                act.activation(th[:, k, :], Z[:, :], ACT.Tanh, scale=0.5)
                                if g >= 2:
                                    act.wait_ge(tl_ok, g - 1)
                                act.activation(tv[:, k, :], Z[:, :], ACT.Copy).then_inc(z_used, 1)
                            yield
                            yield

                    def finish(b):
                        act.wait_ge(o_done, n.next("fin", NCH))
                        act.activation(yT[:, 0, :], ACC[0][:, :], ACT.Copy).then_inc(acc_out, 1)
                        for _ in range(N_FIN):
                            yield

                    def half(b, hf):
                        for i in range(N_PREP):
                            if 1 <= i <= TT:
                                t = i - 1
                                act.wait_ge(qkv_ps, n.next("qkv"))
                                g = n.before("sq")
                                if g >= 2:
                                    act.wait_ge(sq_used, g - 1)
                                act.activation(sq[:, t % 2, :], SC[t % 2][:, 0:3 * HW], ACT.Square).then_inc(sq_ok, 1)
                                act.activation(raw[:, t, :], SC[t % 2][:, 0:3 * HW], ACT.Copy).then_inc(raw_ok, 1)
                            if i >= TT + 6:
                                t = i - TT - 6
                                act.wait_ge(stT_ps, n.next("stT", 2) - 1)
                                act.activation(qT[:, :, t * P:(t + 1) * P],
                                               TP[:, :].rearrange("p (j q) -> p j q", j=HP), ACT.Copy).then_inc(qT_ok, 1)
                            if TT + 4 <= i < 2 * TT + 4:
                                t = i - TT - 4
                                k = n.n.get("st_free", 0) + 2 * (t - 1)
                                if k > 0:
                                    act.wait_ge(stT_ps, k)
                                act.wait_ge(mul_ok, n.next("mul"))
                                for j, st in enumerate((stq[:, t, :, :, :], stk[t % 2])):
                                    part = raw[:, t, j * HW:(j + 1) * HW].rearrange("p (h d) -> p h d", d=HD)
                                    act.activation(st[:, :, HI_OF[j], :], part.unsqueeze(2).broadcast_to([P, HH, 2, HD]),
                                                   ACT.Copy).then_inc(sthi_ok, 1)
                            yield
                        n.next("st_free", 2 * TT)
                        for u in range(NU + 2):
                            if u - 2 in LAST:
                                t = LAST.index(u - 2)
                                act.wait_ge(q2_ps, n.next("q2"))
                                act.activation(qT[:, :, t * P:(t + 1) * P],
                                               TP[:, :].rearrange("p (j q) -> p j q", j=HP), ACT.Copy).then_inc(q2_ok, 1)
                            yield
                        for v in range(NP + 5):
                            if v < NP:
                                h, js = PUNITS[v]
                                w = sum(T - j * P for j in js)
                                if v >= 2:
                                    act.wait_ge(pv_ps, n.n.get("pv", 0) + v - 1)
                                act.wait_ge(pT_ps, n.next("pT"))
                                act.activation(pr[:, v % 2, 0:w], SC[v % 2][:, 0:w], ACT.Exp).then_inc(p_ok, 1)
                            if v == NP // 2 + 2:
                                act.wait_ge(pv_ps, n.n.get("pv", 0) + NP // 2)
                                act.activation(oT[:, 0, :], TP[:, :], ACT.Copy).then_inc(oT_ok, 1)
                            yield
                        n.next("pv", NP)

                    def weights_qkv():
                        act.wait_ge(q_in, 16 * KD)
                        act.activation(wqkv[0][:, :, :], stage_q, ACT.Copy).then_inc(q_hi, 1)

                    round_of_two(norm, route, experts, finish, half, weights_qkv)

                @block.gpsimd
                def _(pool):
                    n = Count()

                    def link(ins):
                        ins.then_inc(self_pool, 1)
                        pool.wait_ge(self_pool, n.next("self"))

                    def weights_qkv():
                        pool.memset(stq[:, :, :, 3, :].bitcast(F32), 0.0).then_inc(q_lo, 1)
                        pool.wait_ge(q_hi, 1)
                        pool.tensor_tensor(wqkv[1][:, :, :], stage_q, wqkv[0][:, :, :].bitcast(F32),
                                           ALU.subtract).then_inc(q_lo, 1)

                    def norm(b):
                        pool.wait_ge(ln_stats, n.next("ln", TT))
                        n.next("xt", KD)
                        link(pool.tensor_scalar(vare[:, :], mv[:, 0, :, 1], LN_EPS, None, ALU.add))
                        pool.tensor_tensor(rstd[:, 0, :], vare[:, :], mhalf[:, :], ALU.pow).then_inc(rstd_ok, 1)
                        for _ in range(N_NORM):
                            yield

                    def route(b):
                        for _ in range(N_ROUTE):
                            yield

                    def experts(b):
                        for _ in range(N_EXPERTS):
                            yield

                    def finish(b):
                        for _ in range(N_FIN):
                            yield

                    def half(b, hf):
                        if hf == 0:
                            pool.wait_ge(xt_ps, n.n["xt"])
                            pool.memset(vx[:, :, :, HD:], 0.0).then_inc(vx_ok, 1)
                            pool.wait_ge(vx_ok, n.next("vx", 2) - 1)
                            pool.memset(vx[:, :, :, HD:HD + 1], 1.0).then_inc(vx_ok, 1)
                        for t in range(0, TT, 2):
                            y, r, sn = (a[:, t:t + 2, :] for a in (nry, nrt, nrm))
                            pool.wait_ge(guess_ok, n.next("guess"))
                            for i in range(3):
                                link(pool.tensor_tensor(r, y, y, ALU.mult))
                                link(pool.tensor_tensor(r, r, sn, ALU.mult))
                                link(pool.tensor_scalar(r, r, -0.5, 1.5, ALU.mult, ALU.add))
                                last = pool.tensor_tensor(y, y, r, ALU.mult)
                                if i < 2:
                                    link(last)
                            last.then_inc(rs_ok, 1)
                        for _ in range(N_PREP + NU + 2 + NP + 5):
                            yield

                    round_of_two(norm, route, experts, finish, half, weights_qkv)

                @block.vector
                def _(dve):
                    n = Count()

                    def link(ins):
                        ins.then_inc(self_dve, 1)
                        dve.wait_ge(self_dve, n.next("self"))

                    def norm(b):
                        if n.n.get("upd", 0):
                            dve.wait_ge(x_upd, n.n["upd"])
                        else:
                            dve.wait_ge(x_in[b], 16)
                        for t in range(TT):
                            last = dve.bn_stats(stats[:, t, :], xs[:, b, t, :])
                        link(last)
                        for t in range(TT):
                            dve.bn_aggr(mv[:, 0, t, :], stats[:, t, :]).then_inc(ln_stats, 1)
                        yield
                        dve.wait_ge(rstd_ok, n.next("rstd"))
                        for t in range(TT):
                            dve.tensor_scalar(xn[:, t, :], xs[:, b, t, :], mv[:, 0, t, 0:1], rstd[:, 0, t:t + 1],
                                              ALU.subtract, ALU.mult).then_inc(xn_ok, 1)
                        yield
                        yield
                        for kk in range(KD):
                            dve.wait_ge(xt_hi, n.next("xt"))
                            dve.tensor_tensor(xTl[b][:, kk, :], SC[kk][:, :], xTh[b][:, kk, :].bitcast(F32),
                                              ALU.subtract).then_inc(xt_lo, 1)
                            yield
                        yield

                    def route(b):
                        flat = score[:, :, :, :].rearrange("p t g e -> p (t g e)")
                        dve.wait_ge(rt_exp, n.next("rt"))
                        link(dve.tensor_scalar(flat, flat, 1.0, None, ALU.add))
                        link(dve.reciprocal(flat, flat))
                        dve.tensor_tensor(pmx[:, :, :, :], score[:, :, :, 0:2], score[:, :, :, 2:4], ALU.max)
                        link(dve.tensor_tensor(pmn[:, :, :, :], score[:, :, :, 0:2], score[:, :, :, 2:4], ALU.min))
                        dve.tensor_tensor(gsum[:, :, :], pmx[:, :, :, 0], pmx[:, :, :, 1], ALU.max)
                        dve.tensor_tensor(gbest[:, :, :], pmx[:, :, :, 0], pmx[:, :, :, 1], ALU.min)
                        link(dve.tensor_tensor(pmn[:, :, :, 0], pmn[:, :, :, 0], pmn[:, :, :, 1], ALU.max))
                        link(dve.tensor_tensor(gbest[:, :, :], gbest[:, :, :], pmn[:, :, :, 0], ALU.max))
                        link(dve.tensor_tensor(gsum[:, :, :], gsum[:, :, :], gbest[:, :, :], ALU.add))
                        yield
                        shape = [P, TT, G, G]
                        other = gsum[:, :, :].unsqueeze(2).broadcast_to(shape)
                        own = gsum[:, :, :].unsqueeze(3).broadcast_to(shape)
                        dve.tensor_tensor(gcmp[:, :, :, :], other, own, ALU.is_gt)
                        link(dve.tensor_tensor(gcm2[:, :, :, :], other, own, ALU.is_ge))
                        link(dve.tensor_tensor(gcm2[:, :, :, :], gcm2[:, :, :, :],
                                               tri[:, :, :].unsqueeze(1).broadcast_to(shape), ALU.mult))
                        link(dve.tensor_tensor(gcmp[:, :, :, :], gcmp[:, :, :, :], gcm2[:, :, :, :], ALU.max))
                        link(dve.tensor_reduce(gbest[:, :, :], gcmp[:, :, :, :], AX_X, ALU.add))
                        link(dve.tensor_scalar(gbest[:, :, :], gbest[:, :, :], 2.0, None, ALU.is_lt))
                        link(dve.tensor_tensor(score[:, :, :, :], score[:, :, :, :],
                                               gbest[:, :, :].unsqueeze(3).broadcast_to([P, TT, G, GS]), ALU.mult))
                        yield
                        rows = score[:, :, :, :].rearrange("p t g e -> p t (g e)")
                        for t in range(TT):
                            link(dve.max(top8[:, t, :], rows[:, t, :]))
                        for t in range(TT):
                            last = dve.max_index(idx8[:, t, :], top8[:, t, :], rows[:, t, :])
                            if t == TT - 1:
                                link(last)
                        yield
                        dve.tensor_copy(idxf[:, :, :], idx8[:, :, 0:TOPK])
                        link(dve.tensor_tensor(wsum[:, :], top8[:, :, 0], top8[:, :, 1], ALU.add))
                        link(dve.tensor_scalar(wsum[:, :], wsum[:, :], TOP_EPS, None, ALU.add))
                        link(dve.reciprocal(wsum[:, :], wsum[:, :]))
                        link(dve.scalar_tensor_tensor(out=wtop[:, :, :], in0=top8[:, :, 0:TOPK], scalar=0.5,
                                                      in1=wsum[:, :].unsqueeze(2).broadcast_to([P, TT, TOPK]),
                                                      op0=ALU.mult, op1=ALU.mult))
                        yield
                        wide = [P, TT, E]
                        for j, c in enumerate((cw, cw2)):
                            link(dve.tensor_tensor(c[:, :, :], iot[:, :].unsqueeze(1).broadcast_to(wide),
                                                   idxf[:, :, j:j + 1].broadcast_to(wide), ALU.is_equal))
                            link(dve.tensor_tensor(c[:, :, :], c[:, :, :], wtop[:, :, j:j + 1].broadcast_to(wide), ALU.mult))
                        link(dve.tensor_tensor(cw[:, :, :], cw[:, :, :], cw2[:, :, :], ALU.add))
                        link(dve.tensor_copy(cc[:, :, 0:E], cw[:, :, :]))
                        dve.tensor_tensor(cc[:, :, E:2 * E], cw[:, :, :], cc[:, :, 0:E].bitcast(F32), ALU.subtract).then_inc(comb_ok, 1)
                        for _ in range(N_ROUTE - 4):
                            yield

                    def experts(b):
                        inst = n.before("experts")
                        for c in range(NCH + 2):
                            g = inst * NCH + c
                            k = g % 2
                            if 1 <= c <= NCH:
                                dve.wait_ge(u_ok, g)
                                if c <= NROUTED:
                                    dve.wait_ge(c_full, n.next("c"))
                                    dve.tensor_tensor(tv[:, 1 - k, :], th[:, 1 - k, :], CWB[:, :], ALU.mult).then_inc(t_ok, 1)
                                else:
                                    dve.tensor_scalar(tv[:, 1 - k, :], th[:, 1 - k, :], 0.5, None, ALU.mult).then_inc(t_ok, 1)
                            yield
                            if 1 <= c <= NCH:
                                dve.wait_ge(t_ok, g)
                                if g >= 3:
                                    dve.wait_ge(o_done, g - 2)
                                dve.tensor_copy(tvh[:, 1 - k, :], tv[:, 1 - k, :]).then_inc(th_ok, 1)
                            if c < NCH:
                                dve.wait_ge(z_used, g + 1)
                                dve.scalar_tensor_tensor(out=th[:, k, :], in0=th[:, k, :], scalar=1.0, in1=tv[:, k, :],
                                                         op0=ALU.add, op1=ALU.mult).then_inc(u_ok, 1)
                            yield
                            if 1 <= c <= NCH:
                                dve.wait_ge(th_ok, g)
                                dve.tensor_tensor(tvl[:, 1 - k, :], tv[:, 1 - k, :], tvh[:, 1 - k, :].bitcast(F32),
                                                  ALU.subtract).then_inc(tl_ok, 1)
                            yield

                    def finish(b):
                        dve.wait_ge(o_done, n.next("fin", NCH))
                        dve.tensor_copy(yT[:, 1, :], ACC[1][:, :]).then_inc(acc_out, 1)
                        yield
                        for j in range(2):
                            dve.wait_ge(fin_ps, n.next("fin_ps"))
                            rows = xs[:, b, 2 * j:2 * j + 2, :].rearrange("p t d -> p (t d)")
                            dve.tensor_tensor(rows, SC[j][:, :], rows, ALU.add).then_inc(x_upd, 1)
                            n.next("upd")
                            yield
                        yield

                    def half(b, hf):
                        def heads(ap):
                            return ap.rearrange("p (h d) -> p h d", d=HD)

                        n.next("raw", TT)
                        for step in range(N_PREP):
                            i = step - 1
                            if 0 <= i < TT:
                                dve.wait_ge(sq_ok, n.next("sq"))
                                dve.tensor_reduce(nrm[:, i, :], heads(sq[:, i % 2, :]), AX_X, ALU.add).then_inc(sq_used, 1)
                                dve.wait_ge(sq_used, n.next("sq_used"))
                                if i == TT - 1:
                                    for st in stk:
                                        dve.memset(st[:, :, 3, :].bitcast(F32), 1.0)
                                    if n.n.get("q2", 0):
                                        dve.wait_ge(q2_ps, n.n["q2"])
                                    else:
                                        dve.wait_ge(q_lo, 1)
                                    dve.memset(stq[:, :, :, 3, 0:1].bitcast(F32), 0.0)
                                if i % 2:
                                    y, sn = (a[:, i - 1:i + 1, :].bitcast(I32) for a in (nry, nrm))
                                    link(dve.tensor_scalar(y, sn, 1, None, ALU.arith_shift_right))
                                    dve.tensor_scalar(y, y, -1.0, float(0x5F3759DF), ALU.mult, ALU.add).then_inc(guess_ok, 1)
                            if i in (TT + 1, TT + 3):
                                two = slice(i - TT - 1, i - TT + 1)
                                r = nrt[:, two, :]
                                dve.wait_ge(rs_ok, n.next("rs"))
                                link(dve.tensor_tensor(r, nry[:, two, :], nrm[:, two, :], ALU.mult))
                                link(dve.tensor_scalar(r, r, L2_EPS, None, ALU.add))
                                link(dve.reciprocal(r, r))
                                link(dve.tensor_scalar(nrt[:, two, 0:HH], nrt[:, two, 0:HH], taub[:, 0:1], None, ALU.mult))
                            if TT + 2 <= i < 2 * TT + 2:
                                t = i - TT - 2
                                dve.wait_ge(raw_ok, n.n["raw"])
                                dve.tensor_tensor(heads(raw[:, t, 0:2 * HW]), heads(raw[:, t, 0:2 * HW]),
                                                  nrt[:, t, 0:2 * HH].unsqueeze(2).broadcast_to([P, 2 * HH, HD]), ALU.mult).then_inc(mul_ok, 1)
                                dve.tensor_tensor(vx[:, t, :, 0:HD], heads(raw[:, t, 2 * HW:]),
                                                  nrt[:, t, 2 * HH:].unsqueeze(2).broadcast_to([P, HH, HD]), ALU.mult)
                            if TT + 4 <= i < 2 * TT + 4:
                                t = i - TT - 4
                                for j, st in enumerate((stq[:, t, :, :, :], stk[t % 2])):
                                    dve.wait_ge(sthi_ok, n.next("sthi"))
                                    part = heads(raw[:, t, j * HW:(j + 1) * HW]).unsqueeze(2)
                                    dve.tensor_tensor(st[:, :, LO_OF[j], :], part, st[:, :, 0:1, :].bitcast(F32),
                                                      ALU.subtract).then_inc(st_ok, 1)
                            if i + 1 >= TT + 6:
                                t = i + 1 - TT - 6
                                dve.wait_ge(stT_ps, n.next("stT", 2))
                                dve.tensor_copy(kT[:, :, t * P:(t + 1) * P],
                                                OV[:, :].rearrange("p (j q) -> p j q", j=HP)).then_inc(kT_ok, 1)
                            yield
                        for u in range(NU + 2):
                            if 1 <= u <= NU:
                                qt, h0, nh = UNITS[u - 1]
                                h = ORDER[h0]
                                dve.wait_ge(sc_ps, n.next("sc"))
                                dve.tensor_reduce(stq[:, qt, h:h + 2 * nh - 1:2, 3, 0],
                                                  MX[(u - 1) % 3][:, 0:nh * (qt + 1) * P].rearrange("p (h w) -> p h w", h=nh),
                                                  AX_X, ALU.max, negate=True).then_inc(max_ok, 1)
                            yield
                        n.next("q2", TT)
                        n.next("pv", NP)
                        for v in range(NP + 5):
                            if v == NP + 2:
                                dve.wait_ge(pv_ps, n.n["pv"])
                                dve.tensor_copy(oT[:, 1, :], OV[:, :]).then_inc(oT_ok, 1)
                            if v == NP + 4:
                                dve.wait_ge(o_ps, n.next("o", 2))
                                sums = [SC[g][:, :].rearrange("p (t h c) -> p t h c", t=TT, h=HG) for g in range(2)]
                                parts = [osum[:, g, :].rearrange("p (t h d) -> p t h d", t=TT, h=HG) for g in range(2)]
                                for g in range(2):
                                    last = dve.reciprocal(rden[:, g, :, :], sums[g][:, :, :, HD])
                                link(last)
                                link(dve.tensor_scalar(rden[:, :, :, :], rden[:, :, :, :], nub[:, 0:1], None, ALU.mult))
                                for g in range(2):
                                    last = dve.tensor_tensor(parts[g], sums[g][:, :, :, 0:HD],
                                                             rden[:, g, :, :].unsqueeze(3).broadcast_to([P, TT, HG, HD]), ALU.mult)
                                link(last)
                                for g in range(2):
                                    rows = xs[:, b, :, hf * HW + g * HW // 2:hf * HW + (g + 1) * HW // 2]
                                    dve.tensor_tensor(rows, rows, osum[:, g, :].rearrange("p (t c) -> p t c", t=TT),
                                                      ALU.add).then_inc(x_upd, 1)
                                    n.next("upd")
                            yield

                    round_of_two(norm, route, experts, finish, half)
            clear()


def kernel(**inputs):
    import concourse.bacc as _bacc
    from concourse.bass_utils import run_bass_kernel_spmd as _run

    a = {k: np.asarray(v) for k, v in inputs.items()}
    pre = "L0_attn_a_"
    mats_a = np.concatenate([a[pre + k] for k in ("w_y", "w_x", "w_ig", "w_ag", "w_out")], axis=1)
    q, k, v = (a["L0_attn_b_" + n].T for n in ("wq", "wk", "wv"))
    w_qkv = np.concatenate([m[:, hf * HW:(hf + 1) * HW] for hf in range(2) for m in (q, k, v)], axis=1)
    w1 = np.zeros((D, HID), np.float32)
    w1[:, 0:E * H] = a["L0_ffn_w1"].transpose(1, 0, 2).reshape(D, E * H)
    w1[:, E * H:(E + 1) * H] = a["L0_ffn_sw1"][0]
    w2 = np.zeros((HID, D), np.float32)
    w2[0:E * H] = a["L0_ffn_w2"].reshape(E * H, D)
    w2[E * H:(E + 1) * H] = a["L0_ffn_sw2"][0]
    rows = [a[pre + k] for k in ("b_y", "b_x", "conv_b", "a_param", "b_ig", "b_ag")] + list(a[pre + "conv_w"])
    vecs = np.stack(rows).reshape(NVEC, 2, P).transpose(2, 0, 1).reshape(P, NVEC * 2)
    sel = np.tile(np.repeat(np.eye(E, dtype=np.float32), H, axis=1), (2, 1))
    arrays = {
        "x": a[pre + "x"], "mats_a": mats_a, "w_qkv": w_qkv, "gate_w": a["L0_ffn_gate_w"].T, "w1": w1, "w2": w2,
        "vecs": vecs, "b_out": a[pre + "b_out"], "tau": a["L0_attn_b_tau"], "nu": a["L0_attn_b_nu"], "sel": sel,
    }
    arrays = {k: np.ascontiguousarray(v) for k, v in arrays.items()}
    nc = _bacc.Bacc("TRN2", target_bir_lowering=False, num_devices=1)
    args = [nc.dram_tensor(k, v.shape, mybir.dt.from_np(v.dtype), kind="ExternalInput").ap() for k, v in arrays.items()]
    out = nc.dram_tensor("out", (B, T, D), F32, kind="ExternalOutput").ap()
    hybrid_kernel(nc, *args, out)
    r = _run(nc, [arrays], core_ids=[0])
    return r.results[0]["out"]
```
